# Optimizing a Trainium2 kernel written in Bass

```python
import numpy as np
import jax
import jax.numpy as jnp

def _softmax(x, axis=-1):
    return jax.nn.softmax(x, axis=axis)

def _gelu(x):
    return jax.nn.gelu(x, approximate=True)

def _silu(x):
    return jax.nn.silu(x)

def _sigmoid(x):
    return jax.nn.sigmoid(x)

def _layernorm(x, axis=-1, eps=1e-05):
    m = jnp.mean(x, axis=axis, keepdims=True)
    v = jnp.var(x, axis=axis, keepdims=True)
    return (x - m) / jnp.sqrt(v + eps)

def _scatter_add(tgt, idx, src, axis=0):
    return tgt.at[idx].add(src)

def _segment_sum(src, seg, n):
    return jax.ops.segment_sum(src, seg, n)
kernel_name = 'mk_gnn_resnorm_d2_gnn_r32_aef2bf'

def setup_inputs(seed: int=0):
    np.random.seed(seed)
    _w = jnp.asarray

    def _rec_inputs():
        import jax
        import jax.numpy as jnp
        _gk = jax.random.key(seed)
        x = -7.329e-05 + 0.9999 * jax.random.normal(jax.random.fold_in(_gk, 1), (50000, 256), jnp.float32)
        src = jax.random.randint(jax.random.fold_in(_gk, 2), (25000,), 0, 50000, jnp.int32)
        dst = jnp.minimum((50000 * jax.random.uniform(jax.random.fold_in(_gk, 3), (25000,)) ** 2.0).astype(jnp.int32), 49999)
        _o = jnp.argsort(dst, stable=True)
        src = src[_o]
        dst = dst[_o]
        edge_attr_64 = -9.77346e-05 + 0.999888 * jax.random.normal(jax.random.fold_in(_gk, 12), (25000, 64), jnp.float32)
        return (x, src, dst, edge_attr_64)
    x, src, dst, edge_attr_64 = _rec_inputs()

    def _L0_gnn_setup():
        import jax, jax.numpy as jnp
        import numpy as np
        DIM = 256
        HIDDEN = 256
        NUM_ENT = 6250
        NUM_TRI = 6250
        NUM_EDGES = 18750
        key = jax.random.key(seed)
        k1, k2, k3, k4, k5 = jax.random.split(key, 5)
        entity_emb = jax.random.normal(k1, (NUM_ENT, DIM), dtype=jnp.float32)
        src_idx = jax.random.randint(k2, (NUM_EDGES,), 0, NUM_ENT, dtype=jnp.int64)
        dst_idx = jax.random.randint(k3, (NUM_EDGES,), 0, NUM_TRI, dtype=jnp.int64)
        entity_triangle_index = jnp.stack([src_idx, dst_idx], axis=0)
        bound = 1.0 / np.sqrt(DIM)
        W = jax.random.uniform(k4, (HIDDEN, DIM), minval=-bound, maxval=bound, dtype=jnp.float32)
        b = jax.random.uniform(k5, (HIDDEN,), minval=-bound, maxval=bound, dtype=jnp.float32)
        return {'entity_emb': entity_emb, 'entity_triangle_index': entity_triangle_index, 'num_triangles': NUM_TRI, 'W': W, 'b': b}
    _L0_gnn_all = _L0_gnn_setup()
    _L0_gnn_in = {k: v for k, v in _L0_gnn_all.items() if k in ('W', 'b')}
    del _L0_gnn_all

    def _L1_gnn_setup():
        import jax, jax.numpy as jnp
        import numpy as np
        ALPHA = 0.2
        key = jax.random.key(seed)
        ks = jax.random.split(key, 6)
        N, E, F_IN, F_OUT, E_DIM = (50000, 25000, 256, 256, 64)
        h = jax.random.normal(ks[0], (N, F_IN), dtype=jnp.float32)
        e_feat = jax.random.normal(ks[1], (E, E_DIM), dtype=jnp.float32)
        W = jax.random.normal(ks[2], (F_OUT, F_IN), dtype=jnp.float32) * (1.0 / np.sqrt(F_IN))
        A = jax.random.normal(ks[3], (1, 2 * F_OUT + E_DIM), dtype=jnp.float32) * 0.05
        src = jax.random.randint(ks[4], (E,), 0, N, dtype=jnp.int32)
        dst = jax.random.randint(ks[5], (E,), 0, N, dtype=jnp.int32)
        return {'h': h, 'e_feat': e_feat, 'W': W, 'A': A, 'src': src, 'dst': dst}
    _L1_gnn_all = _L1_gnn_setup()
    _L1_gnn_in = {k: v for k, v in _L1_gnn_all.items() if k in ('W', 'A')}
    del _L1_gnn_all
    return {'x': x, 'src': src, 'dst': dst, 'edge_attr_64': edge_attr_64, 'L0_gnn_W': _L0_gnn_in['W'], 'L0_gnn_b': _L0_gnn_in['b'], 'L1_gnn_W': _L1_gnn_in['W'], 'L1_gnn_A': _L1_gnn_in['A']}

def reference(x, src, dst, edge_attr_64, L0_gnn_W, L0_gnn_b, L1_gnn_W, L1_gnn_A):
    import jax
    import jax.numpy as jnp

    def _L0_gnn_ref(entity_emb, entity_triangle_index, num_triangles, W, b):
        import jax, jax.numpy as jnp
        import numpy as np
        DIM = 256
        HIDDEN = 256
        NUM_ENT = 6250
        NUM_TRI = 6250
        NUM_EDGES = 18750
        src_idx = entity_triangle_index[0]
        dst_idx = entity_triangle_index[1]
        msgs = entity_emb[src_idx]
        agg = jax.ops.segment_sum(msgs, dst_idx, num_segments=num_triangles)
        counts = jax.ops.segment_sum(jnp.ones((src_idx.shape[0],), dtype=entity_emb.dtype), dst_idx, num_segments=num_triangles)
        agg = jnp.where(counts[:, None] > 0, agg / jnp.maximum(counts, 1.0)[:, None], agg)
        tri_out = jax.nn.relu(agg @ W.T + b)
        return tri_out

    def _L1_gnn_ref(h, e_feat, W, A, src, dst):
        import jax, jax.numpy as jnp
        import numpy as np
        ALPHA = 0.2
        N = h.shape[0]
        F_OUT = W.shape[0]
        z = h @ W.T
        z_src = z[src]
        z_dst = z[dst]
        a_src, a_dst, a_e = (A[0, :F_OUT], A[0, F_OUT:2 * F_OUT], A[0, 2 * F_OUT:])
        logits = z_src @ a_src + z_dst @ a_dst + e_feat @ a_e
        e = jax.nn.leaky_relu(logits, ALPHA)
        m = jax.ops.segment_max(e, dst, num_segments=N)
        ex = jnp.exp(e - m[dst])
        denom = jax.ops.segment_sum(ex, dst, num_segments=N)
        alpha = ex / denom[dst]
        h_out = jax.ops.segment_sum(alpha[:, None] * z_src, dst, num_segments=N)
        return h_out
    edge_index = jnp.stack([src, dst])
    x = _layernorm(x + _L0_gnn_ref(x, edge_index, 50000, L0_gnn_W, L0_gnn_b), axis=-1)
    x = _layernorm(x + _L1_gnn_ref(x, edge_attr_64, L1_gnn_W, L1_gnn_A, src, dst), axis=-1)
    return x

_drawn_inputs = setup_inputs


def setup_inputs(seed=0):
    import zlib

    import numpy as np

    out = dict(_drawn_inputs(seed))
    spreads = {}
    factors = {'L0_gnn_b': 2.703}
    for name, (base, spread) in spreads.items():
        noise = np.random.default_rng([zlib.crc32(name.encode()), seed]).standard_normal(out[name].shape)
        drawn = base * np.exp(spread * noise) if base else spread * noise
        out[name] = jnp.asarray(drawn.astype(out[name].dtype))
    for name, factor in factors.items():
        out[name] = (out[name] * factor).astype(out[name].dtype)
    return out
```

```python
from contextlib import ExitStack

import numpy as np

import concourse.bass as bass
from concourse import mybir

F32 = mybir.dt.float32
BF16 = mybir.dt.bfloat16
I32 = mybir.dt.int32
ALU = mybir.AluOpType
ACT = mybir.ActivationFunctionType

P = 128
N, D, E, DE = 50000, 256, 25000, 64
HALVES = D // P
GT = 7
TILES = 196
GROUPS = TILES // GT
GE = GT * P
EPAD = TILES * P
HT = TILES // 2
RB = 14
BLOCK = P * RB
LAST_BLOCK = N - BLOCK
EPS = 1e-5
ALPHA = 0.2
BIG = 1e37
PAD_DST = 65535
FAR = 65536
CODE = P + 1
assert BLOCK * (GROUPS - 1) < N <= BLOCK * GROUPS and GROUPS % 2 == 0 and TILES == GROUPS * GT
DMA = 16


def gnn_kernel(nc, x, src_lane, src_line, dst_line, dst_lane, dst_next_lane, dst_carry_lane,
               dst_rows, dst_prev_rows, dst_next_rows, dst_up_rows, dst_up_next_rows, code_step,
               attr_t, w0_t, w1_t, w1, b0, att, out):
    table = nc.dram_tensor("row_table", (N + EPAD, D), F32).ap()
    by_edge = nc.dram_tensor("rows_by_edge", (GROUPS, P, GT * D), F32).ap()
    x_blocks = x[0:BLOCK * (GROUPS - 1), :].rearrange("(g p r) d -> g p (r d)", p=P, r=RB)
    t_blocks = table[0:BLOCK * (GROUPS - 1), :].rearrange("(g p r) d -> g p (r d)", p=P, r=RB)
    o_blocks = out[0:BLOCK * (GROUPS - 1), :].rearrange("(g p r) d -> g p (r d)", p=P, r=RB)
    rep_blocks = table[N:N + EPAD, :].rearrange("(g p k) d -> g p (k d)", p=P, k=GT)
    src_groups = src_line.rearrange("(g e) -> g e", e=GE)
    dst_groups = dst_line.rearrange("(g e) -> g e", e=GE)
    attr_groups = attr_t.rearrange("f (g e) -> g f e", e=GE)

    def block_of(blocks, whole, g):
        if isinstance(g, int) and g == GROUPS - 1:
            return whole[LAST_BLOCK:N, :].rearrange("(p r) d -> p (r d)", r=RB)
        return blocks[g]

    ctx = ExitStack()
    with ctx:
        def sb(name, shape, dt=F32):
            return ctx.enter_context(nc.sbuf_tensor(name, shape, dt))

        def ps(name, shape, dt=F32):
            return ctx.enter_context(nc.psum_tensor(name, shape, dt))

        def sem(name):
            return ctx.enter_context(nc.semaphore(name))

        def pair(name):
            return [sem(f"{name}{s}") for s in range(2)]

        w0_sb = sb("w0_sb", [P, HALVES, D])
        b0_all = sb("b0_all", [P, D])
        relu_b0 = sb("relu_b0", [P, D])
        u_src = sb("u_src", [P, D])
        u_dst = sb("u_dst", [P, D])
        u_sum = sb("u_sum", [P, 1])
        ident = sb("ident", [P, P])
        lane_code = sb("lane_code", [P, P])
        att_cols = sb("att_cols", [P, 4])
        att_edge = sb("att_edge", [DE, 1])
        src_idx = sb("src_idx", [P, TILES], I32)
        rep_idx = sb("rep_idx", [P, TILES], I32)
        row_idx = sb("row_idx", [P, TILES], I32)
        dst_l = sb("dst_l", [P, TILES], I32)
        carry_l = sb("carry_l", [P, TILES], I32)
        src_next1 = sb("src_next1", [P, TILES])
        rep_l = sb("rep_l", [P, TILES])
        per_count = sb("per_count", [P, TILES])
        match_l = sb("match_l", [P, TILES])
        code_l = sb("code_l", [P, TILES])
        dst_score = sb("dst_score", [P, TILES])
        logit_l = sb("logit_l", [P, TILES])
        weight_l = sb("weight_l", [P, TILES])
        per_total = sb("per_total", [P, TILES])
        src_rows_sb = sb("src_rows_sb", [P, 2, GT, D])
        dst_rows_sb = sb("dst_rows_sb", [P, 2, GT, D])
        dst_line_sb = sb("dst_line_sb", [P, 2, GE], I32)
        src_line_sb = sb("src_line_sb", [HT, 2, GE], I32)
        same = sb("same", [P, 2, GE])
        carries = sb("carries", [P, 2, GE])
        below = sb("below", [HT, 2, 2, GE], BF16)
        sums_t = sb("sums_t", [P, 2, D])
        proj = sb("proj", [P, 2 * GT, D])
        scrap = sb("scrap", [P, GT, D], BF16)
        idx_now = sb("idx_now", [P, 2, 2, GT], I32)
        e_stats = sb("e_stats", [P, GT, 6])
        e_twice = sb("e_twice", [P, GT])
        e_gap = sb("e_gap", [P, GT])
        e_sq = sb("e_sq", [P, GT])
        e_part = sb("e_part", [P, GT])
        e_var = sb("e_var", [P, GT])
        e_inv = sb("e_inv", [P, GT])
        e_rstd = sb("e_rstd", [P, GT])
        e_bias = sb("e_bias", [P, GT])
        e_dot = sb("e_dot", [P, 2, GT])
        e_tmp = sb("e_tmp", [P, GT])
        tile_first = sb("tile_first", [HT, 2])
        keep_f, keep_r, lead_f, lead_r = (sb(n, [HT, 2, P])[:] for n in ("keep_f", "keep_r", "lead_f", "lead_r"))
        step_hi = sb("step_hi", [HT, 2, CODE], BF16)
        step_lo = sb("step_lo", [HT, 2, CODE], BF16)
        XB = RB * D
        arena = sb("arena", [P, 6 * XB])
        x_in = arena[:, 0:2 * XB].rearrange("p (s r d) -> p s r d", s=2, r=RB)
        x_one = arena[:, 2 * XB:4 * XB].rearrange("p (s r d) -> p s r d", s=2, r=RB)
        x_two = arena[:, 4 * XB:6 * XB].rearrange("p (s r d) -> p s r d", s=2, r=RB)
        n_stats = sb("n_stats", [P, RB, 6])
        n_twice = sb("n_twice", [P, RB])
        n_gap = sb("n_gap", [P, RB])
        n_sq = sb("n_sq", [P, RB])
        n_part = sb("n_part", [P, RB])
        n_var = sb("n_var", [P, 2, RB])
        n_inv = sb("n_inv", [P, 2, RB])
        n_rstd = sb("n_rstd", [P, 2, RB])
        n_bias = sb("n_bias", [P, 2, RB])

        taken = [0]

        def view(parts, *shape):
            n = int(np.prod(shape))
            a = arena[0:parts, taken[0]:taken[0] + n]
            taken[0] += n
            if len(shape) == 2:
                a = a.rearrange("p (a b) -> p a b", a=shape[0])
            return a

        def rows(parts=HT):
            return view(parts, 2, P)
        a_dst, a_prev, a_next, a_up, a_up_next = (rows().bitcast(I32) for _ in range(5))
        ban_f, ban_r, nolead_f, nolead_r = rows(), rows(), rows(), rows()
        r_a, r_b, r_c, r_d, r_e, r_f = (rows() for _ in range(6))
        zeros_r, ones_r = rows(), rows()
        r_int, r_int2 = rows().bitcast(I32), rows().bitcast(I32)
        code_sb = view(HT, 2, 2)
        whole = view(1, 4, TILES)
        chain_row = view(1, TILES + 2)
        l_a, l_b = view(P, TILES), view(P, TILES)
        l_next, l_src = (view(P, TILES).bitcast(I32) for _ in range(2))
        w1_nat = view(P, HALVES, D)
        w1_sb = view(P, HALVES, D)
        dst_float = view(P, TILES)
        attr_sb = view(DE, 2, GE)
        att_wide = view(P, 4, P)

        ps_t = ps("ps_t", [P, 2, 512])
        ps_y = ps("ps_y", [P, 2, 512])
        ps_d = ps("ps_d", [P, 3, 512])
        ps_m = ps("ps_m", [P, 512])

        loaded = sem("loaded")
        consts_ready = sem("consts_ready")
        dve_step = sem("dve_step")
        wide_ready = sem("wide_ready")
        u_ready = sem("u_ready")
        tails_ready = sem("tails_ready")
        tails_row = sem("tails_row")
        chain_ready = sem("chain_ready")
        chain_cols = sem("chain_cols")
        flip_ready = sem("flip_ready")
        flipped = sem("flipped")
        exp_ready = sem("exp_ready")
        exp_done = sem("exp_done")
        setup_done = sem("setup_done")
        gathers_open = sem("gathers_open")
        x_loaded = pair("x_loaded")
        one_stored = pair("one_stored")
        two_stored = pair("two_stored")
        x_shifted, n_stat, n_aggr, n_vars = sem("x_shifted"), sem("n_stat"), sem("n_aggr"), sem("n_vars")
        n_inv_ready, n_rstd_ready, n_bias_ready = sem("n_inv_ready"), sem("n_rstd_ready"), sem("n_bias_ready")
        x_normed = sem("x_normed")
        search_ready, match_done = sem("search_ready"), sem("match_done")
        row_loaded = pair("row_loaded")
        row_kept = pair("row_kept")
        row_staged, row_dotted, logit_done = sem("row_staged"), sem("row_dotted"), sem("logit_done")
        attr_loaded = pair("attr_loaded")
        attr_done = sem("attr_done")

        class Layer:

            def __init__(self, tag):
                self.line_loaded = pair(tag + "_line_loaded")
                self.src_loaded = pair(tag + "_src_loaded")
                self.dst_loaded = pair(tag + "_dst_loaded")
                self.stored = pair(tag + "_stored")
                self.select_ready = sem(tag + "_select_ready")
                self.t_ready = sem(tag + "_t_ready")
                self.t_copied = sem(tag + "_t_copied")
                self.y_ready = sem(tag + "_y_ready")
                self.y_copied = sem(tag + "_y_copied")
                self.y_used = sem(tag + "_y_used")
                self.summed = sem(tag + "_summed")
                self.stat = sem(tag + "_stat")
                self.aggr = sem(tag + "_aggr")
                self.vars = sem(tag + "_vars")
                self.inv_ready = sem(tag + "_inv_ready")
                self.rstd_ready = sem(tag + "_rstd_ready")
                self.bias_ready = sem(tag + "_bias_ready")
                self.normed = sem(tag + "_normed")
                self.staged = sem(tag + "_staged")

        one, two = Layer("a"), Layer("b")

        block = ctx.enter_context(nc.Block())

        SETUP_LOADS = 15

        @block.sync
        def _(sp):
            for dst, src in (
                (w0_sb[:], w0_t.rearrange("(h p) n -> p h n", p=P)),
                (w1_nat, w1.rearrange("(h p) n -> p h n", p=P)),
                (b0_all[:], b0.partition_broadcast(P)),
                (att_cols[:], att[0:2 * D].rearrange("(c p) -> p c", p=P)),
                (att_edge[:], att[2 * D:2 * D + DE].rearrange("(p c) -> p c", c=1)),
                (src_idx[:], src_lane), (dst_l[:], dst_lane), (carry_l[:], dst_carry_lane),
                (l_next, dst_next_lane), (a_dst, dst_rows), (a_prev, dst_prev_rows),
                (a_next, dst_next_rows), (a_up, dst_up_rows), (a_up_next, dst_up_next_rows),
                (code_sb, code_step),
            ):
                sp.dma_start(dst, src, allow_slow_non_contiguous=True).then_inc(loaded, DMA)
            sp.wait_ge(setup_done, 1)

            def load_line(ly, g, s, first, with_src):
                if not first:
                    sp.wait_ge(ly.select_ready, g - 1)
                sp.dma_start(dst_line_sb[:, s, :], dst_groups[g].partition_broadcast(P)).then_inc(ly.line_loaded[s], DMA)
                if with_src:
                    sp.dma_start(src_line_sb[:, s, :], src_groups[g].partition_broadcast(HT)).then_inc(ly.line_loaded[s], DMA)

            def load_x(g, s):
                sp.dma_start(x_in[:, s].rearrange("p r d -> p (r d)"), block_of(x_blocks, x, g)).then_inc(x_loaded[s], DMA)

            def store_x(g, s):
                sp.wait_ge(x_normed, g + 1)
                if isinstance(g, int) and g == GROUPS - 1:
                    sp.wait_ge(one_stored[1 - s], DMA * GROUPS // 2)
                    sp.wait_ge(two_stored[1 - s], DMA * GROUPS // 2)
                sp.dma_start(block_of(t_blocks, table[0:N, :], g), x_one[:, s].rearrange("p r d -> p (r d)")).then_inc(one_stored[s], DMA)
                sp.dma_start(block_of(o_blocks, out, g), x_two[:, s].rearrange("p r d -> p (r d)")).then_inc(two_stored[s], DMA)

            def store_rep(g, s):
                sp.wait_ge(one.normed, g + 1)
                sp.dma_start(rep_blocks[g], dst_rows_sb[:, s].rearrange("p k d -> p (k d)")).then_inc(one.stored[s], DMA)

            for g in range(2):
                load_x(g, g)
                load_line(one, g, g, True, True)
            store_x(0, 0)
            load_x(2, 0)
            load_line(one, 2, 0, False, True)
            with sp.Fori(0, (GROUPS - 4) // 2) as i:
                for s in (1, 0):
                    g = 2 * i + (3 if s else 4)
                    store_x(g - 2, s)
                    load_x(g, s)
                    load_line(one, g, s, False, True)
                    store_rep(g - 3, 1 - s)
            g = GROUPS - 1
            store_x(g - 2, 1)
            load_x(g, 1)
            load_line(one, g, 1, False, True)
            store_rep(g - 3, 0)
            store_x(g - 1, 0)
            store_rep(g - 2, 1)
            store_x(g, 1)
            store_rep(g - 1, 0)
            store_rep(g, 1)

            def load_attr(g, s):
                sp.dma_start(attr_sb[:, s, :], attr_groups[g]).then_inc(attr_loaded[s], DMA)

            def keep(g, s, it):
                sp.wait_ge(row_loaded[s], GT * DMA * (it + 1))
                sp.dma_start(by_edge[g], src_rows_sb[:, s].rearrange("p k d -> p (k d)")).then_inc(row_kept[s], DMA)

            for s in range(2):
                sp.wait_ge(one_stored[s], DMA * GROUPS // 2)
                sp.wait_ge(two_stored[s], DMA * GROUPS // 2)
            sp.dma_start(w1_sb, w1_t.rearrange("(h p) n -> p h n", p=P)).then_inc(loaded, DMA)
            load_attr(0, 0)
            load_attr(1, 1)
            with sp.Fori(0, GROUPS // 2 - 1) as i:
                for s in range(2):
                    keep(2 * i + s, s, i)
                    sp.wait_ge(attr_done, 2 * i + s + 1)
                    load_attr(2 * i + s + 2, s)
            for s in range(2):
                keep(GROUPS - 2 + s, s, GROUPS // 2 - 1)

            def load_two(g, s, it, first):
                load_line(two, g, s, first, False)
                if not first:
                    sp.wait_ge(two.t_ready, GT * (g - 1))
                sp.dma_start(src_rows_sb[:, s].rearrange("p k d -> p (k d)"), by_edge[g]).then_inc(two.src_loaded[s], DMA)
                if not first:
                    sp.wait_ge(two.stored[s], GT * DMA * it)
                sp.dma_start(dst_rows_sb[:, s].rearrange("p k d -> p (k d)"), rep_blocks[g]).then_inc(two.dst_loaded[s], DMA)

            for s in range(2):
                sp.wait_ge(row_kept[s], DMA * GROUPS // 2)
                sp.wait_ge(one.stored[s], DMA * GROUPS // 2)
            sp.wait_ge(row_dotted, GROUPS)
            for s in range(2):
                load_two(s, s, 0, True)
            with sp.Fori(1, GROUPS // 2) as i:
                for s in range(2):
                    load_two(2 * i + s, s, i, False)

        @block.gpsimd
        def _(pool):
            nc.gpsimd.memset(ident[:], 0.0).then_inc(consts_ready, 1)
            nc.gpsimd.memset(dst_rows_sb[:], 0.0).then_inc(consts_ready, 1)
            nc.gpsimd.memset(zeros_r, 0.0).then_inc(consts_ready, 1)
            nc.gpsimd.memset(ones_r, 1.0).then_inc(consts_ready, 1)
            nc.gpsimd.iota(lane_code[:], [[GT, P]], base=1, channel_multiplier=0,
                           allow_small_or_imprecise_dtypes=True).then_inc(consts_ready, 1)
            pool.wait_ge(consts_ready, 5)
            nc.gpsimd.affine_select(out=ident[:], in_=ident[:], compare_op=ALU.not_equal, fill=1.0,
                                    base=0, pattern=[[-1, P]], channel_multiplier=1).then_inc(consts_ready, 1)
            pool.wait_ge(setup_done, 1)

            def gather(dst, src, idx, k, bound, done_sem):
                pool.indirect_dma_start(
                    out=dst, out_offset=None, in_=src,
                    in_offset=bass.IndirectOffsetOnAxis(ap=idx[:, k:k + 1], axis=0),
                    bounds_check=bound, oob_is_err=False).then_inc(done_sem, DMA)

            def gather_one(g, s, it, first):
                if not first:
                    pool.wait_ge(one.src_loaded[s], GT * DMA * it)
                    pool.wait_ge(one.dst_loaded[s], GT * DMA * it)
                nc.gpsimd.tensor_copy(idx_now[:, s, 0, :], src_idx[:, bass.ds(g * GT, GT)]).then_inc(one.staged, 1)
                nc.gpsimd.tensor_copy(idx_now[:, s, 1, :], rep_idx[:, bass.ds(g * GT, GT)]).then_inc(one.staged, 1)
                if not first:
                    pool.wait_ge(one.t_ready, GT * (g - 1))
                pool.wait_ge(one.staged, 2 * g + 2)
                pool.sem_inc(gathers_open, 1)
                for k in range(GT):
                    gather(src_rows_sb[:, s, k, :], x, idx_now[:, s, 0], k, N - 1, one.src_loaded[s])
                if not first:
                    pool.wait_ge(one.stored[s], DMA * it)
                    pool.sem_inc(gathers_open, 1)
                for k in range(GT):
                    gather(dst_rows_sb[:, s, k, :], x, idx_now[:, s, 1], k, N - 1, one.dst_loaded[s])

            for s in range(2):
                gather_one(s, s, 0, True)
            with pool.Fori(1, GROUPS // 2) as i:
                for s in range(2):
                    gather_one(2 * i + s, s, i, False)

            for s in range(2):
                pool.wait_ge(one_stored[s], DMA * GROUPS // 2)
                pool.wait_ge(one.stored[s], DMA * GROUPS // 2)
            pool.wait_ge(match_done, GROUPS + 1)

            def gather_row(g, s, it, first):
                if not first:
                    pool.wait_ge(row_loaded[s], GT * DMA * it)
                nc.gpsimd.tensor_copy(idx_now[:, s, 0, :], row_idx[:, bass.ds(g * GT, GT)]).then_inc(row_staged, 1)
                if not first:
                    pool.wait_ge(row_kept[s], DMA * it)
                    pool.wait_ge(row_dotted, g - 1)
                pool.wait_ge(row_staged, g + 1)
                pool.sem_inc(gathers_open, 1)
                for k in range(GT):
                    gather(src_rows_sb[:, s, k, :], table, idx_now[:, s, 0], k, N + EPAD - 1, row_loaded[s])

            pool.wait_ge(one.t_ready, TILES)
            for s in range(2):
                pool.wait_ge(one.src_loaded[s], GT * DMA * GROUPS // 2)
                pool.wait_ge(one.dst_loaded[s], GT * DMA * GROUPS // 2)
            for s in range(2):
                gather_row(s, s, 0, True)
            with pool.Fori(1, GROUPS // 2) as i:
                for s in range(2):
                    gather_row(2 * i + s, s, i, False)

            for s in range(2):
                pool.wait_ge(two_stored[s], DMA * GROUPS // 2)
                pool.wait_ge(row_loaded[s], GT * DMA * GROUPS // 2)

            def scatter(g, s, it, first):
                if not first:
                    pool.wait_ge(two.stored[s], GT * DMA * it)
                nc.gpsimd.tensor_copy(idx_now[:, s, 1, :], rep_idx[:, bass.ds(g * GT, GT)]).then_inc(two.staged, 1)
                pool.wait_ge(two.staged, g + 1)
                pool.wait_ge(two.normed, g + 1)
                pool.sem_inc(gathers_open, 1)
                for k in range(GT):
                    pool.indirect_dma_start(
                        out=out, out_offset=bass.IndirectOffsetOnAxis(ap=idx_now[:, s, 1, k:k + 1], axis=0),
                        in_=dst_rows_sb[:, s, k, :], in_offset=None,
                        bounds_check=N - 1, oob_is_err=False).then_inc(two.stored[s], DMA)

            for s in range(2):
                scatter(s, s, 0, True)
            with pool.Fori(1, GROUPS // 2) as i:
                for s in range(2):
                    scatter(2 * i + s, s, i, False)
            for s in range(2):
                pool.wait_ge(two.stored[s], GT * DMA * GROUPS // 2)

        @block.tensor
        def _(pe):
            pe.wait_ge(wide_ready, 1)
            for j in range(2):
                for h in range(HALVES):
                    last = nc.tensor.matmul(ps_y[:, j, 0:D], att_wide[:, 2 * j + h, :], w1_nat[:, h, :],
                                            start=h == 0, stop=h == HALVES - 1)
            last.then_inc(u_ready, 1)

            def scan_turns(n, row, tail):
                pe.wait_ge(tails_ready, n + 1)
                for h in range(2):
                    last = nc.tensor.transpose(ps_m[0:1, h * HT:(h + 1) * HT], row[:, h, tail:tail + 1], ident[0:HT, 0:HT])
                last.then_inc(tails_row, 1)
                off = 0 if tail else 1
                pe.wait_ge(chain_ready, n + 1)
                for h in range(2):
                    last = nc.tensor.transpose(ps_m[0:HT, 256 + h:257 + h], chain_row[:, off + h * HT:off + (h + 1) * HT],
                                               ident[0:1, 0:1])
                last.then_inc(chain_cols, 1)

            def to_lanes(n, row):
                pe.wait_ge(flip_ready, n + 1)
                for h in range(2):
                    last = nc.tensor.transpose(ps_m[:, h * HT:(h + 1) * HT], row[:, h, :], ident[0:HT, 0:HT])
                last.then_inc(flipped, 1)

            def to_rows(n, lanes):
                pe.wait_ge(flip_ready, n + 1)
                for h in range(2):
                    last = nc.tensor.transpose(ps_m[0:HT, h * P:(h + 1) * P], lanes[:, h * HT:(h + 1) * HT], ident[:])
                last.then_inc(flipped, 1)

            def wholes_to_row(n):
                pe.wait_ge(flip_ready, n + 1)
                for j, (row, tail) in enumerate(((lead_f, P - 1), (lead_r, 0))):
                    for h in range(2):
                        last = nc.tensor.transpose(ps_m[0:1, j * TILES + h * HT:j * TILES + (h + 1) * HT],
                                                   row[:, h, tail:tail + 1], ident[0:HT, 0:HT])
                last.then_inc(flipped, 1)

            wholes_to_row(0)
            scan_turns(0, r_a, P - 1)
            to_lanes(1, r_f)

            def search(g, s, first):
                pe.wait_ge(one.select_ready, g + 1)
                if not first:
                    pe.wait_ge(match_done, g)
                for k in range(GT):
                    into = ps_d[:, k // 3, k % 3 * CODE:(k % 3 + 1) * CODE]
                    for n, (h, step) in enumerate(((0, step_hi), (0, step_lo), (1, step_hi), (1, step_lo))):
                        last = nc.tensor.matmul(into, below[:, h, s, k * P:(k + 1) * P], step[:, h, :],
                                                start=n == 0, stop=n == 3)
                last.then_inc(search_ready, 1)

            def add_up(ly, w, g, s, loads, it, first):
                pe.wait_ge(ly.select_ready, g + 1)
                pe.wait_ge(ly.src_loaded[s], loads * (it + 1))

                def sums(k):
                    slot = (GT * s + k) % 2
                    if not (first and k < 2):
                        pe.wait_ge(ly.t_copied, GT * g + k - 1)
                    for h in range(HALVES):
                        last = nc.tensor.matmul(ps_t[:, slot, h * P:(h + 1) * P], src_rows_sb[:, s, k, h * P:(h + 1) * P],
                                                same[:, s, k * P:(k + 1) * P], start=True, stop=True)
                    last.then_inc(ly.t_ready, 1)

                def project(k):
                    slot = (GT * s + k) % 2
                    very_first = first and k == 0
                    pe.wait_ge(ly.t_copied, GT * g + k + 1)
                    if not (first and k < 2):
                        pe.wait_ge(ly.y_copied, GT * g + k - 1)
                    for h in range(HALVES):
                        last = nc.tensor.matmul(ps_y[:, slot, 0:D], sums_t[:, slot, h * P:(h + 1) * P], w[:, h, :],
                                                start=h == 0, stop=very_first and h == HALVES - 1)
                    if not very_first:
                        pe.wait_ge(ly.y_copied, GT * g + k)
                        last = nc.tensor.matmul(ps_y[:, slot, 0:D], carries[:, s, k * P:(k + 1) * P],
                                                proj[:, (GT * s + k - 1) % (2 * GT), :], start=False, stop=True)
                    last.then_inc(ly.y_ready, 1)

                sums(0)
                for k in range(1, GT):
                    sums(k)
                    project(k - 1)
                project(GT - 1)

            search(0, 0, True)
            add_up(one, w0_sb, 0, 0, GT * DMA, 0, True)
            search(1, 1, False)
            add_up(one, w0_sb, 1, 1, GT * DMA, 0, False)
            with pe.Fori(1, GROUPS // 2) as i:
                for s in range(2):
                    search(2 * i + s, s, False)
                    add_up(one, w0_sb, 2 * i + s, s, GT * DMA, i, False)

            def attr_logits(g, s, it):
                pe.wait_ge(attr_loaded[s], DMA * (it + 1))
                if not isinstance(g, int):
                    pe.wait_ge(logit_done, g - 1)
                for k in range(GT):
                    last = nc.tensor.matmul(ps_d[:, s, k:k + 1], attr_sb[:, s, k * P:(k + 1) * P], att_edge[:],
                                            start=True, stop=True)
                last.then_inc(attr_done, 1)

            pe.wait_ge(match_done, GROUPS)
            for s in range(2):
                attr_logits(s, s, 0)
            with pe.Fori(1, GROUPS // 2) as i:
                for s in range(2):
                    attr_logits(2 * i + s, s, i)

            wholes_to_row(2)
            to_rows(3, l_a)
            scan_turns(1, r_b, 0)
            to_rows(4, l_b)
            scan_turns(2, r_d, P - 1)
            scan_turns(3, r_e, 0)
            scan_turns(4, r_f, P - 1)
            to_lanes(5, r_a)
            to_lanes(6, r_b)

            add_up(two, w1_sb, 0, 0, DMA, 0, True)
            add_up(two, w1_sb, 1, 1, DMA, 0, False)
            with pe.Fori(1, GROUPS // 2) as i:
                for s in range(2):
                    add_up(two, w1_sb, 2 * i + s, s, DMA, i, False)

        @block.scalar
        def _(act):
            def copy_sums(ly, g, s, k):
                slot = (GT * s + k) % 2
                act.wait_ge(ly.t_ready, GT * g + k + 1)
                nc.scalar.copy(sums_t[:, slot, :], ps_t[:, slot, 0:D]).then_inc(ly.t_copied, 1)

            def copy_proj(ly, g, s, k):
                act.wait_ge(ly.y_ready, GT * g + k + 1)
                nc.scalar.copy(proj[:, GT * s + k, :], ps_y[:, (GT * s + k) % 2, 0:D]).then_inc(ly.y_copied, 1)

            def copies(ly, g, s, k):
                copy_sums(ly, g, s, k)
                if k:
                    copy_proj(ly, g, s, k - 1)
                if k == GT - 1:
                    copy_proj(ly, g, s, k)

            def node_rstd(g):
                act.wait_ge(x_normed, g)
                act.wait_ge(n_inv_ready, g + 1)
                nc.scalar.activation(n_rstd[:], n_inv[:], ACT.Sqrt).then_inc(n_rstd_ready, 1)

            def node_norm(g, s, it, r):
                if r == 0:
                    act.wait_ge(n_bias_ready, g + 1)
                    act.wait_ge(one_stored[s], DMA * it)
                    act.wait_ge(two_stored[s], DMA * it)
                nc.scalar.activation(x_one[:, s, r, :], x_in[:, s, r, :], ACT.Identity,
                                     bias=n_bias[:, 0, r:r + 1], scale=n_rstd[:, 0, r:r + 1])
                last = nc.scalar.activation(x_two[:, s, r, :], x_in[:, s, r, :], ACT.Identity,
                                            bias=n_bias[:, 1, r:r + 1], scale=n_rstd[:, 1, r:r + 1])
                if r == RB - 1:
                    last.then_inc(x_normed, 1)

            def edge_rstd(ly, g):
                act.wait_ge(ly.normed, g)
                act.wait_ge(ly.inv_ready, g + 1)
                nc.scalar.activation(e_rstd[:], e_inv[:], ACT.Sqrt).then_inc(ly.rstd_ready, 1)

            def edge_norm(ly, g, s):
                act.wait_ge(ly.bias_ready, g + 1)
                for k in range(GT):
                    last = nc.scalar.activation(dst_rows_sb[:, s, k, :], proj[:, GT * s + k, :], ACT.Identity,
                                                bias=e_bias[:, k:k + 1], scale=e_rstd[:, k:k + 1])
                last.then_inc(ly.normed, 1)

            def turn_one(g, s, it, first=False, last=False):
                node_rstd(g)
                if not first:
                    edge_norm(one, g - 1, 1 - s)
                for k in range(GT):
                    node_norm(g, s, it, 2 * k)
                    node_norm(g, s, it, 2 * k + 1)
                    if not last:
                        copies(one, g + 1, 1 - s, k)
                edge_rstd(one, g)

            act.wait_ge(setup_done, 1)
            for k in range(GT):
                copies(one, 0, 0, k)
            turn_one(0, 0, 0, first=True)
            with act.Fori(0, GROUPS // 2 - 1) as i:
                turn_one(2 * i + 1, 1, i)
                turn_one(2 * i + 2, 0, i + 1)
            turn_one(GROUPS - 1, 1, GROUPS // 2 - 1, last=True)
            edge_norm(one, GROUPS - 1, 1)

            act.wait_ge(exp_ready, 1)
            nc.scalar.activation(r_e, r_e, ACT.Exp).then_inc(exp_done, 1)

            for s in range(2):
                act.wait_ge(one.stored[s], DMA * GROUPS // 2)

            def turn_two(g, s, first=False, last=False):
                if not first:
                    edge_norm(two, g - 1, 1 - s)
                if not last:
                    for k in range(GT):
                        copies(two, g + 1, 1 - s, k)
                edge_rstd(two, g)

            for k in range(GT):
                copies(two, 0, 0, k)
            turn_two(0, 0, first=True)
            with act.Fori(0, GROUPS // 2 - 1) as i:
                turn_two(2 * i + 1, 1)
                turn_two(2 * i + 2, 0)
            turn_two(GROUPS - 1, 1, last=True)
            edge_norm(two, GROUPS - 1, 1)

        @block.vector
        def _(dve):
            v = nc.vector
            steps = [0]

            def link(ins):
                steps[0] += 1
                ins.then_inc(dve_step, 1)
                dve.wait_ge(dve_step, steps[0])

            def link_all(instructions):
                for ins in instructions:
                    steps[0] += 1
                    ins.then_inc(dve_step, 1)
                dve.wait_ge(dve_step, steps[0])

            def seg_scan(n, vals, into, reverse, biggest):
                flags = (ban_r if reverse else ban_f) if biggest else (keep_r if reverse else keep_f)
                leads = (nolead_r if reverse else nolead_f) if biggest else (lead_r if reverse else lead_f)
                whole_row = whole[:, 2 * biggest + reverse, :]
                start = -BIG if biggest else 0.0
                op0, op1 = (ALU.add, ALU.max) if biggest else (ALU.mult, ALU.add)
                way = slice(None, None, -1) if reverse else slice(None)
                for h in range(2):
                    last = v.tensor_tensor_scan(into[:, h, way], flags[:, h, way], vals[:, h, way], start, op0, op1)
                last.then_inc(tails_ready, 1)
                row = chain_row[:, 0:TILES] if reverse else chain_row[:, 1:TILES + 1]
                link(v.memset(chain_row[:, TILES:TILES + 1] if reverse else chain_row[:, 0:1], start))
                dve.wait_ge(tails_row, n + 1)
                v.tensor_tensor_scan(row[:, way], whole_row[:, way], ps_m[0:1, 0:TILES][:, way], start,
                                     op0, op1).then_inc(chain_ready, 1)
                dve.wait_ge(chain_cols, n + 1)
                link_all(v.scalar_tensor_tensor(into[:, h, :], leads[:, h, :], ps_m[0:HT, 256 + h:257 + h],
                                                into[:, h, :], op0, op1) for h in range(2))

            def copy_wholes(n):
                dve.wait_ge(flipped, n + 1)
                for j in range(2):
                    v.tensor_copy(whole[:, j, :], ps_m[0:1, j * TILES:(j + 1) * TILES])
                link_all(v.tensor_scalar(whole[:, 2 + j, :], ps_m[0:1, j * TILES:(j + 1) * TILES], 1.0, BIG,
                                         ALU.subtract, ALU.mult) for j in range(2))

            dve.wait_ge(loaded, SETUP_LOADS * DMA)
            dve.wait_ge(consts_ready, 6)
            link_all((
                v.tensor_scalar(relu_b0[:], b0_all[:], 0.0, None, ALU.max),
                v.tensor_tensor(keep_f, a_dst, a_prev, ALU.is_equal),
                v.tensor_tensor(keep_r, a_dst, a_next, ALU.is_equal),
                v.tensor_tensor(rep_l[:], dst_l[:], l_next, ALU.not_equal),
                v.tensor_scalar(src_next1[:], src_idx[:], 1.0, None, ALU.add),
                v.tensor_copy(tile_first[:], a_dst[:, :, 0]),
                v.tensor_scalar(r_b, a_dst, 1.0, None, ALU.add),
                v.tensor_scalar(r_c, a_up, 1.0, None, ALU.add),
                v.tensor_tensor(r_d, a_dst, a_next, ALU.not_equal),
                v.tensor_tensor(r_e, a_up, a_up_next, ALU.not_equal),
            ))
            v.tensor_copy(att_wide, att_cols[:].unsqueeze(2).to_broadcast([P, 4, P])).then_inc(wide_ready, 1)
            link_all(v.tensor_tensor_scan(into[:, h, way], keep[:, h, way], zeros_r[:, h, :], 1.0, ALU.mult, ALU.add)
                     for into, keep, way in ((lead_f, keep_f, slice(None)), (lead_r, keep_r, slice(None, None, -1)))
                     for h in range(2))
            v.memset(l_b, 0.0).then_inc(flip_ready, 1)
            link_all((v.tensor_tensor(r_b, r_b, r_d, ALU.mult), v.tensor_tensor(r_c, r_c, r_e, ALU.mult)))
            link(v.tensor_tensor(r_b, r_b, r_c, ALU.subtract))
            link(v.tensor_copy(r_int, r_b))
            link(v.tensor_single_scalar(r_int2, r_int, 255, ALU.bitwise_and))
            link(v.tensor_copy(r_c, r_int2))
            link_all((
                v.tensor_tensor(step_hi[:, :, 0:P], r_b, r_c, ALU.subtract),
                v.tensor_copy(step_lo[:, :, 0:P], r_c),
                v.tensor_copy(step_hi[:, :, P], code_sb[:, :, 0]),
                v.tensor_copy(step_lo[:, :, P], code_sb[:, :, 1]),
                v.tensor_scalar(l_a, rep_l[:], -1.0, -float(FAR), ALU.add, ALU.mult),
            ))
            link(v.tensor_tensor(rep_idx[:], l_a, dst_l[:], ALU.add))
            copy_wholes(0)
            seg_scan(0, ones_r, r_a, 0, 0)
            v.tensor_copy(r_f, r_a).then_inc(flip_ready, 1)
            dve.wait_ge(flipped, 2)
            link(v.reciprocal(per_count[:], ps_m[:, 0:TILES]))
            dve.wait_ge(u_ready, 1)
            link_all((v.tensor_copy(u_src[:], ps_y[:, 0, 0:D]), v.tensor_copy(u_dst[:], ps_y[:, 1, 0:D])))
            v.reduce_sum(u_sum[:], u_dst[:], axis=mybir.AxisListType.X).then_inc(setup_done, 1)
            dve.wait_ge(setup_done, 1)

            def cols(a, g):
                return a[:, bass.ds(g * GT, GT)]

            def col(a, g, k):
                return a[:, bass.ds(g * GT + k, 1)]

            def equal_lines(into, g, s, lanes):
                return v.tensor_tensor(into[:, s, :].rearrange("p (k e) -> p k e", k=GT),
                                       dst_line_sb[:, s, :].rearrange("p (k e) -> p k e", k=GT),
                                       cols(lanes, g).unsqueeze(2).to_broadcast([P, GT, P]), ALU.is_equal)

            def selectors(g, s, it, first=False):
                dve.wait_ge(one.line_loaded[s], 2 * DMA * (it + 1))
                if not first:
                    dve.wait_ge(one.y_ready, GT * (g - 1))
                    dve.wait_ge(search_ready, g - 1)
                equal_lines(same, g, s, dst_l)
                equal_lines(carries, g, s, carry_l)
                for h in range(2):
                    last = v.tensor_scalar(below[:, h, s, :], src_line_sb[:, s, :], tile_first[:, h:h + 1], None, ALU.is_ge)
                last.then_inc(one.select_ready, 1)

            def aggregate(stats, twice, gap, sq, part, stat, aggr, g):
                dve.wait_ge(stat, g + 1)
                v.tensor_tensor(twice[:], stats[:, :, 1], stats[:, :, 4], ALU.add)
                v.tensor_tensor(sq[:], stats[:, :, 2], stats[:, :, 5], ALU.add)
                v.tensor_tensor(gap[:], stats[:, :, 1], stats[:, :, 4], ALU.subtract).then_inc(aggr, 1)
                dve.wait_ge(aggr, 3 * g + 1)
                v.scalar_tensor_tensor(gap[:], gap[:], 0.25, gap[:], ALU.mult, ALU.mult).then_inc(aggr, 1)
                dve.wait_ge(aggr, 3 * g + 2)
                v.scalar_tensor_tensor(part[:], sq[:], 1.0 / D, gap[:], ALU.mult, ALU.add).then_inc(aggr, 1)
                dve.wait_ge(aggr, 3 * g + 3)

            def node_stats(g, s, it):
                dve.wait_ge(x_loaded[s], DMA * (it + 1))
                v.tensor_tensor(x_in[:, s], x_in[:, s], relu_b0[:].unsqueeze(1).to_broadcast([P, RB, D]),
                                ALU.add).then_inc(x_shifted, 1)
                dve.wait_ge(x_shifted, g + 1)
                for r in range(RB):
                    last = v.bn_stats(n_stats[:, r, :], x_in[:, s, r, :])
                last.then_inc(n_stat, 1)
                aggregate(n_stats, n_twice, n_gap, n_sq, n_part, n_stat, n_aggr, g)
                v.tensor_scalar(n_var[:, 0, :], n_part[:], EPS, None, ALU.add)
                v.tensor_scalar(n_var[:, 1, :], n_part[:], 1.0 + EPS, EPS * EPS, ALU.mult, ALU.add).then_inc(n_vars, 1)
                dve.wait_ge(n_vars, g + 1)
                v.reciprocal(n_inv[:], n_var[:]).then_inc(n_inv_ready, 1)

            def node_bias(g):
                dve.wait_ge(n_rstd_ready, g + 1)
                v.scalar_tensor_tensor(n_bias[:], n_twice[:].unsqueeze(1).to_broadcast([P, 2, RB]), -0.5, n_rstd[:],
                                       ALU.mult, ALU.mult).then_inc(n_bias_ready, 1)

            def finish_stats(ly, g, s):
                for k in range(GT):
                    last = v.bn_stats(e_stats[:, k, :], proj[:, s * GT + k, :])
                last.then_inc(ly.stat, 1)
                aggregate(e_stats, e_twice, e_gap, e_sq, e_part, ly.stat, ly.aggr, g)
                v.tensor_scalar(e_var[:], e_part[:], EPS, None, ALU.add).then_inc(ly.vars, 1)
                dve.wait_ge(ly.vars, g + 1)
                v.reciprocal(e_inv[:], e_var[:]).then_inc(ly.inv_ready, 1)

            def finish_bias(ly, g):
                dve.wait_ge(ly.rstd_ready, g + 1)
                v.scalar_tensor_tensor(e_bias[:], e_twice[:], -0.5, e_rstd[:], ALU.mult, ALU.mult).then_inc(ly.bias_ready, 1)

            def finish_one(g, s, it, last_group=False):
                dve.wait_ge(one.y_copied, GT * (g + 1))
                if not last_group:
                    dve.wait_ge(one.y_ready, GT * (g + 1) + 1)
                for k in range(GT):
                    row = proj[:, s * GT + k, :]
                    last = v.scalar_tensor_tensor(row, row, col(per_count, g, k), b0_all[:],
                                                  ALU.mult, ALU.add)
                last.then_inc(one.y_used, 1)
                dve.wait_ge(one.dst_loaded[s], GT * DMA * (it + 1))
                dve.wait_ge(one.y_used, g + 1)
                for k in range(GT):
                    row = proj[:, s * GT + k, :]
                    last = v.scalar_tensor_tensor(row, row, 0.0, dst_rows_sb[:, s, k, :], ALU.max, ALU.add)
                last.then_inc(one.summed, 1)
                dve.wait_ge(one.summed, g + 1)
                for k in range(GT):
                    v.tensor_tensor_reduce(out=scrap[:, k, :], in0=proj[:, s * GT + k, :], in1=u_dst[:], scale=1.0, scalar=0.0,
                                           op0=ALU.mult, op1=ALU.add, accum_out=e_dot[:, 0, k:k + 1])
                finish_stats(one, g, s)

            def score_one(g):
                dve.wait_ge(one.rstd_ready, g + 1)
                v.tensor_tensor(e_tmp[:], e_dot[:, 0, :], e_rstd[:], ALU.mult)
                finish_bias(one, g)
                dve.wait_ge(one.bias_ready, g + 1)
                v.scalar_tensor_tensor(cols(dst_score, g), e_bias[:], u_sum[:], e_tmp[:], ALU.mult, ALU.add)

            def match(g):
                dve.wait_ge(search_ready, g + 1)
                for k in range(GT):
                    at = k % 3 * CODE
                    v.scalar_tensor_tensor(scrap[:, k, 0:P], ps_d[:, k // 3, at:at + P], col(src_next1, g, k), lane_code[:],
                                           ALU.is_equal, ALU.mult, accum_out=col(match_l, g, k))
                v.tensor_copy(code_l[:, bass.ds(g * GT, 6)].rearrange("p (a b) -> p a b", b=3),
                              ps_d[:, 0:2, 0:3 * CODE].rearrange("p a (b c) -> p a b c", c=CODE)[:, :, :, P])
                v.tensor_copy(col(code_l, g, 6), ps_d[:, 2, P:P + 1]).then_inc(match_done, 1)

            def turn_one(g, s, it, first=False, last=False):
                node_stats(g, s, it)
                if not first:
                    score_one(g - 1)
                if not last:
                    selectors(g + 1, 1 - s, it + 1 if s else it)
                node_bias(g)
                finish_one(g, s, it, last)
                if not last:
                    match(g + 1)

            selectors(0, 0, 0, True)
            match(0)
            turn_one(0, 0, 0, first=True)
            with dve.Fori(0, GROUPS // 2 - 1) as i:
                turn_one(2 * i + 1, 1, i)
                turn_one(2 * i + 2, 0, i + 1)
            turn_one(GROUPS - 1, 1, GROUPS // 2 - 1, last=True)

            link_all((v.tensor_scalar(weight_l[:], match_l[:], 0.0, None, ALU.is_gt),
                      v.scalar_tensor_tensor(per_total[:], match_l[:], -1.0, code_l[:], ALU.add, ALU.add)))
            link(v.tensor_tensor(per_total[:], per_total[:], src_idx[:], ALU.subtract))
            link(v.tensor_tensor(per_total[:], per_total[:], weight_l[:], ALU.mult))
            v.tensor_tensor(row_idx[:], per_total[:], src_idx[:], ALU.add).then_inc(match_done, 1)
            score_one(GROUPS - 1)

            def dots(g, s, it, first):
                dve.wait_ge(row_loaded[s], GT * DMA * (it + 1))
                if not first:
                    dve.wait_ge(logit_done, g)
                for k in range(GT):
                    last = v.tensor_tensor_reduce(out=scrap[:, k, :], in0=src_rows_sb[:, s, k, :], in1=u_src[:], scale=1.0,
                                                  scalar=0.0, op0=ALU.mult, op1=ALU.add, accum_out=e_dot[:, s, k:k + 1])
                last.then_inc(row_dotted, 1)
                dve.wait_ge(row_dotted, g + 1)
                dve.wait_ge(attr_done, g + 1)
                v.tensor_tensor(cols(logit_l, g), e_dot[:, s, :], ps_d[:, s, 0:GT], ALU.add).then_inc(logit_done, 1)

            for s in range(2):
                dots(s, s, 0, s == 0)
            with dve.Fori(1, GROUPS // 2) as i:
                for s in range(2):
                    dots(2 * i + s, s, i, False)
            dve.wait_ge(logit_done, GROUPS)

            for s in range(2):
                dve.wait_ge(one_stored[s], DMA * GROUPS // 2)
                dve.wait_ge(two_stored[s], DMA * GROUPS // 2)
            link_all([v.tensor_scalar(ban, keep, 1.0, BIG, ALU.subtract, ALU.mult)
                      for ban, keep in ((ban_f, keep_f), (ban_r, keep_r), (nolead_f, lead_f), (nolead_r, lead_r))]
                     + [v.tensor_tensor(l_a, dst_score[:], rep_l[:], ALU.mult), v.tensor_copy(l_b, logit_l[:]),
                        v.tensor_copy(dst_float, dst_l[:])])
            v.memset(r_f, 0.0).then_inc(flip_ready, 1)
            copy_wholes(2)

            def rows_of_ps():
                return ps_m[0:HT, 0:2 * P].rearrange("p (h e) -> p h e", h=2)

            v.memset(r_c, 0.0).then_inc(flip_ready, 1)
            dve.wait_ge(flipped, 4)
            link(v.tensor_copy(r_a, rows_of_ps()))
            seg_scan(1, r_a, r_b, 1, 0)
            v.memset(r_d, 0.0).then_inc(flip_ready, 1)
            dve.wait_ge(flipped, 5)
            link(v.tensor_tensor(r_c, rows_of_ps(), r_b, ALU.add))
            link(v.scalar_tensor_tensor(r_c, r_c, ALPHA, r_c, ALU.mult, ALU.max))
            seg_scan(2, r_c, r_d, 0, 1)
            seg_scan(3, r_c, r_e, 1, 1)
            link(v.tensor_tensor(r_d, r_d, r_e, ALU.max))
            v.tensor_tensor(r_e, r_c, r_d, ALU.subtract).then_inc(exp_ready, 1)
            dve.wait_ge(exp_done, 1)
            seg_scan(4, r_e, r_f, 0, 0)
            v.tensor_copy(r_a, r_e).then_inc(flip_ready, 1)
            dve.wait_ge(flipped, 6)
            link(v.tensor_copy(weight_l[:], ps_m[:, 0:TILES]))
            v.tensor_copy(r_b, r_f).then_inc(flip_ready, 1)
            dve.wait_ge(flipped, 7)
            link(v.scalar_tensor_tensor(per_total[:], ps_m[:, 0:TILES], -1.0, rep_l[:], ALU.add, ALU.mult))
            link(v.tensor_scalar(per_total[:], per_total[:], 1.0, None, ALU.add))
            link(v.reciprocal(per_total[:], per_total[:]))

            def selectors_two(g, s, it, first=False):
                dve.wait_ge(two.line_loaded[s], DMA * (it + 1))
                if not first:
                    dve.wait_ge(two.y_ready, GT * (g - 1))
                for k in range(GT):
                    v.tensor_scalar(same[:, s, k * P:(k + 1) * P], dst_line_sb[:, s, k * P:(k + 1) * P],
                                    col(dst_float, g, k), col(weight_l, g, k), ALU.is_equal, ALU.mult)
                equal_lines(carries, g, s, carry_l).then_inc(two.select_ready, 1)

            def finish_two(g, s, it, last_group=False):
                dve.wait_ge(two.y_copied, GT * (g + 1))
                if not last_group:
                    dve.wait_ge(two.y_ready, GT * (g + 1) + 1)
                dve.wait_ge(two.dst_loaded[s], DMA * (it + 1))
                for k in range(GT):
                    row = proj[:, s * GT + k, :]
                    last = v.scalar_tensor_tensor(row, row, col(per_total, g, k), dst_rows_sb[:, s, k, :],
                                                  ALU.mult, ALU.add)
                last.then_inc(two.summed, 1)
                dve.wait_ge(two.summed, g + 1)
                finish_stats(two, g, s)

            def turn_two(g, s, it, first=False, last=False):
                if not first:
                    finish_bias(two, g - 1)
                if not last:
                    selectors_two(g + 1, 1 - s, it + 1 if s else it)
                finish_two(g, s, it, last)

            selectors_two(0, 0, 0, True)
            turn_two(0, 0, 0, first=True)
            with dve.Fori(0, GROUPS // 2 - 1) as i:
                turn_two(2 * i + 1, 1, i)
                turn_two(2 * i + 2, 0, i + 1)
            turn_two(GROUPS - 1, 1, GROUPS // 2 - 1, last=True)
            finish_bias(two, GROUPS - 1)


def kernel(x, src, dst, edge_attr_64, L0_gnn_W, L0_gnn_b, L1_gnn_W, L1_gnn_A):
    import concourse.bacc as bacc
    from concourse.bass_utils import run_bass_kernel_spmd

    def padded(a, before, after):
        return np.concatenate([np.asarray(before, np.int32),
                               np.asarray(a, np.int32), np.asarray(after, np.int32)])

    def lanes(line):
        return np.ascontiguousarray(line.reshape(TILES, P).T)

    def rows(line):
        return np.ascontiguousarray(line.reshape(2, HT, P).transpose(1, 0, 2))

    src, dst = np.asarray(src), np.asarray(dst)
    src_line = padded(src, [], [0] * (EPAD - E))
    dst_line = padded(dst, [], [PAD_DST] * (EPAD - E))
    dst_next = np.append(dst_line[1:], np.int32(-1))
    dst_prev = np.insert(dst_line[:-1], 0, np.int32(-1))
    dst_up = np.concatenate([np.full(P, -1, np.int32), dst_line[:-P]])
    dst_up_next = np.concatenate([np.full(P, -1, np.int32), dst_next[:-P]])
    dst_carry = np.full((P, TILES), -1, np.int32)
    dst_carry[P - 1, 1:] = dst_line[P - 1:-P:P]
    code = N + np.arange(TILES) // GT * GE + np.arange(TILES) % GT
    step = np.diff(code, prepend=0)
    code_step = np.stack([step // 256 * 256, step % 256], -1).astype(np.float32).reshape(2, HT, 2).transpose(1, 0, 2)
    attr_t = np.concatenate([np.asarray(edge_attr_64).T, np.zeros((DE, EPAD - E), np.float32)], 1)
    w0, w1 = np.asarray(L0_gnn_W), np.asarray(L1_gnn_W)
    arrays = {
        "x": np.asarray(x), "src_lane": lanes(src_line), "src_line": src_line, "dst_line": dst_line,
        "dst_lane": lanes(dst_line), "dst_next_lane": lanes(dst_next), "dst_carry_lane": dst_carry,
        "dst_rows": rows(dst_line), "dst_prev_rows": rows(dst_prev), "dst_next_rows": rows(dst_next),
        "dst_up_rows": rows(dst_up), "dst_up_next_rows": rows(dst_up_next),
        "code_step": np.ascontiguousarray(code_step), "attr_t": np.ascontiguousarray(attr_t),
        "w0_t": np.ascontiguousarray(w0.T), "w1_t": np.ascontiguousarray(w1.T), "w1": w1,
        "b0": np.asarray(L0_gnn_b), "att": np.asarray(L1_gnn_A)[0],
    }
    nc = bacc.Bacc("TRN2", target_bir_lowering=False, num_devices=1)
    args = [nc.dram_tensor(name, a.shape, mybir.dt.from_np(a.dtype), kind="ExternalInput").ap()
            for name, a in arrays.items()]
    out = nc.dram_tensor("out", (N, D), F32, kind="ExternalOutput").ap()
    gnn_kernel(nc, *args, out)
    r = run_bass_kernel_spmd(nc, [arrays], core_ids=[0])
    return r.results[0]["out"]
```

```python
from contextlib import ExitStack

import numpy as np

import concourse.bass as bass
from concourse import mybir

F32 = mybir.dt.float32
BF16 = mybir.dt.bfloat16
I32 = mybir.dt.int32
ALU = mybir.AluOpType
ACT = mybir.ActivationFunctionType

P = 128
N, D, E, DE = 50000, 256, 25000, 64
HALVES = D // P
GT = 7
TILES = 196
GROUPS = TILES // GT
GE = GT * P
EPAD = TILES * P
HT = TILES // 2
RB = 14
HB = RB // 2
BLOCK = P * RB
LAST_BLOCK = N - BLOCK
EPS = 1e-5
ALPHA = 0.2
BIG = 1e37
PAD_DST = 65535
FAR = 65536
CODE = P + 1
assert BLOCK * (GROUPS - 1) < N <= BLOCK * GROUPS and GROUPS % 2 == 0 and TILES == GROUPS * GT
DMA = 16


def gnn_kernel(nc, x, src_lane, src_line, dst_line, dst_lane, dst_next_lane, dst_rows, dst_prev_rows, dst_next_rows, dst_up_rows, dst_up_next_rows, code_step,
               attr_lane, w0_t, w1_t, w1, b0, att, out):
    table = nc.dram_tensor("row_table", (N + EPAD, D), F32).ap()
    by_edge = nc.dram_tensor("rows_by_edge", (GROUPS, P, GT * D), F32).ap()
    lead_line = nc.dram_tensor("lead_line", (EPAD,), F32).ap()
    x_blocks = x[0:BLOCK * (GROUPS - 1), :].rearrange("(g p r) d -> g p (r d)", p=P, r=RB)
    t_blocks = table[0:BLOCK * (GROUPS - 1), :].rearrange("(g p r) d -> g p (r d)", p=P, r=RB)
    o_blocks = out[0:BLOCK * (GROUPS - 1), :].rearrange("(g p r) d -> g p (r d)", p=P, r=RB)
    rep_blocks = table[N:N + EPAD, :].rearrange("(g p k) d -> g p (k d)", p=P, k=GT)
    src_groups = src_line.rearrange("(g e) -> g e", e=GE)
    dst_groups = dst_line.rearrange("(g e) -> g e", e=GE)
    lead_groups = lead_line.rearrange("(g o e) -> g o e", o=1, e=GE)
    attr_groups = attr_lane.rearrange("p (g k) f -> g p (k f)", k=GT)

    def block_of(blocks, whole, g, half):
        if isinstance(g, int) and g == GROUPS - 1:
            return whole[LAST_BLOCK:N, :].rearrange("(p r) d -> p (r d)", r=RB)[:, half * HB * D:(half + 1) * HB * D]
        return blocks[g][:, half * HB * D:(half + 1) * HB * D]

    def is_group(g):
        return not isinstance(g, int) or 0 <= g < GROUPS

    def wait(engine, semaphore, count):
        if not isinstance(count, int) or count > 0:
            engine.wait_ge(semaphore, count)

    def every_group(engine, turn, apart=2):
        for g in (0, 1):
            turn(g, g, 0)
        with engine.Fori(1, (GROUPS - apart) // 2) as i:
            for s in range(2):
                turn(2 * i + s, s, i)
        for g in range(GROUPS - apart, GROUPS):
            turn(g, g % 2, g // 2)

    ctx = ExitStack()
    with ctx:
        def sb(name, shape, dt=F32):
            return ctx.enter_context(nc.sbuf_tensor(name, shape, dt))

        def ps(name, shape, dt=F32):
            return ctx.enter_context(nc.psum_tensor(name, shape, dt))

        def sem(name):
            return ctx.enter_context(nc.semaphore(name))

        def pair(name):
            return [sem(f"{name}{s}") for s in range(2)]

        w0_sb = sb("w0_sb", [P, HALVES, D])
        b0_all = sb("b0_all", [P, D])
        relu_b0 = sb("relu_b0", [P, D])
        u_src = sb("u_src", [P, D])
        u_dst = sb("u_dst", [P, D])
        u_sum = sb("u_sum", [P, 1])
        ident = sb("ident", [P, P])
        lane_code = sb("lane_code", [P, P])
        att_cols = sb("att_cols", [P, 4])
        att_edge = sb("att_edge", [P, DE])
        src_idx = sb("src_idx", [P, TILES], I32)
        rep_idx = sb("rep_idx", [P, TILES], I32)
        row_idx = sb("row_idx", [P, TILES], I32)
        dst_l = sb("dst_l", [P, TILES], I32)
        src_next1 = sb("src_next1", [P, TILES])
        rep_l = sb("rep_l", [P, TILES])
        per_count = sb("per_count", [P, TILES])
        match_l = sb("match_l", [P, TILES])
        code_l = sb("code_l", [P, TILES])
        dst_score = sb("dst_score", [P, TILES])
        logit_l = sb("logit_l", [P, TILES])
        weight_l = sb("weight_l", [P, TILES])
        per_total = sb("per_total", [P, TILES])
        src_rows_sb = sb("src_rows_sb", [P, 2, GT, D])
        dst_rows_sb = sb("dst_rows_sb", [P, 2, GT, D])
        dst_line_sb = sb("dst_line_sb", [P, 2, GE], I32)
        src_line_sb = sb("src_line_sb", [HT, 2, GE], I32)
        same = sb("same", [P, 2, GE])
        carries = sb("carries", [P, 2, GE])
        below = sb("below", [HT, 2, 2, GE], BF16)
        sums_t = sb("sums_t", [P, 2, D])
        proj = sb("proj", [P, 2 * GT, D])
        carried = sb("carried", [P, 2, D])
        scrap = sb("scrap", [P, GT, D], BF16)
        idx_now = sb("idx_now", [P, 2, 2, GT], I32)
        e_stats = sb("e_stats", [P, GT, 6])
        e_twice = sb("e_twice", [P, GT])
        e_gap = sb("e_gap", [P, GT])
        e_sq = sb("e_sq", [P, GT])
        e_part = sb("e_part", [P, GT])
        e_var = sb("e_var", [P, GT])
        e_inv = sb("e_inv", [P, GT])
        e_rstd = sb("e_rstd", [P, GT])
        e_bias = sb("e_bias", [P, GT])
        e_dot = sb("e_dot", [P, 2, GT])
        e_tmp = sb("e_tmp", [P, GT])
        tile_first = sb("tile_first", [HT, 2])
        keep_f, keep_r, lead_f, lead_r = (sb(n, [HT, 2, P])[:] for n in ("keep_f", "keep_r", "lead_f", "lead_r"))
        step_hi = sb("step_hi", [HT, 2, CODE], BF16)
        step_lo = sb("step_lo", [HT, 2, CODE], BF16)
        XB = RB * D
        arena = sb("arena", [P, 6 * XB])
        x_in = arena[:, 0:2 * XB].rearrange("p (s r d) -> p s r d", s=2, r=RB)
        x_one = arena[:, 2 * XB:4 * XB].rearrange("p (s r d) -> p s r d", s=2, r=RB)
        x_two = arena[:, 4 * XB:6 * XB].rearrange("p (s r d) -> p s r d", s=2, r=RB)
        n_stats = sb("n_stats", [P, RB, 6])
        n_twice = sb("n_twice", [P, RB])
        n_gap = sb("n_gap", [P, RB])
        n_sq = sb("n_sq", [P, RB])
        n_part = sb("n_part", [P, RB])
        n_var = sb("n_var", [P, 2, RB])
        n_inv = sb("n_inv", [P, 2, RB])
        n_rstd = sb("n_rstd", [P, 2, RB])
        n_bias = sb("n_bias", [P, 2, RB])

        taken = [0]

        def view(parts, *shape):
            n = int(np.prod(shape))
            a = arena[0:parts, taken[0]:taken[0] + n]
            taken[0] += n
            if len(shape) == 2:
                a = a.rearrange("p (a b) -> p a b", a=shape[0])
            return a

        def rows(parts=HT):
            return view(parts, 2, P)
        a_dst, a_prev, a_next, a_up, a_up_next = (rows().bitcast(I32) for _ in range(5))
        ban_f, ban_r, nolead_f, nolead_r = rows(), rows(), rows(), rows()
        r_a, r_b, r_c, r_d, r_e, r_f = (rows() for _ in range(6))
        zeros_r, ones_r = rows(), rows()
        r_int, r_int2 = rows().bitcast(I32), rows().bitcast(I32)
        code_sb = view(HT, 2, 2)
        whole = view(1, 4, TILES)
        chain_row = view(1, TILES + 2)
        l_a, l_b = view(P, TILES), view(P, TILES)
        l_next, l_src = (view(P, TILES).bitcast(I32) for _ in range(2))
        w1_nat = view(P, HALVES, D)
        w1_sb = view(P, HALVES, D)
        dst_float = view(P, TILES)
        attr_sb = view(P, 2, GT * DE)
        att_wide = view(P, 4, P)
        finished = view(P, 2 * GT, D)

        ps_t = ps("ps_t", [P, 2, 512])
        ps_y = ps("ps_y", [P, 2, 512])
        ps_d = ps("ps_d", [P, 3, 512])
        ps_m = ps("ps_m", [P, 512])

        loaded = sem("loaded")
        consts_ready = sem("consts_ready")
        dve_step = sem("dve_step")
        wide_ready = sem("wide_ready")
        u_ready = sem("u_ready")
        tails_ready = sem("tails_ready")
        tails_row = sem("tails_row")
        chain_ready = sem("chain_ready")
        chain_cols = sem("chain_cols")
        flip_ready = sem("flip_ready")
        flipped = sem("flipped")
        exp_ready = sem("exp_ready")
        exp_done = sem("exp_done")
        leads_ready = sem("leads_ready")
        leads_stored = sem("leads_stored")
        setup_done = sem("setup_done")
        src_staged = sem("src_staged")
        gathers_open = sem("gathers_open")
        moves_open = sem("moves_open")
        x_loaded = pair("x_loaded")
        one_stored = pair("one_stored")
        two_stored = pair("two_stored")
        x_shifted, n_stat, n_aggr, n_vars = sem("x_shifted"), sem("n_stat"), sem("n_aggr"), sem("n_vars")
        n_inv_ready, n_rstd_ready, n_bias_ready = sem("n_inv_ready"), sem("n_rstd_ready"), sem("n_bias_ready")
        x_normed = sem("x_normed")
        search_ready, match_done = sem("search_ready"), sem("match_done")
        row_loaded = pair("row_loaded")
        row_kept = pair("row_kept")
        row_staged, row_dotted, logit_done = sem("row_staged"), sem("row_dotted"), sem("logit_done")
        row_turned = sem("row_turned")
        row_turn_copied = sem("row_turn_copied")
        row_projecting = sem("row_projecting")
        row_projected = sem("row_projected")
        attr_loaded = pair("attr_loaded")
        attr_scaled = sem("attr_scaled")

        class Layer:

            def __init__(self, tag):
                self.line_loaded = pair(tag + "_line_loaded")
                self.src_loaded = pair(tag + "_src_loaded")
                self.dst_loaded = pair(tag + "_dst_loaded")
                self.stored = pair(tag + "_stored")
                self.select_ready = sem(tag + "_select_ready")
                self.t_ready = sem(tag + "_t_ready")
                self.t_copied = sem(tag + "_t_copied")
                self.y_ready = sem(tag + "_y_ready")
                self.y_copied = sem(tag + "_y_copied")
                self.y_used = sem(tag + "_y_used")
                self.summed = sem(tag + "_summed")
                self.stat = sem(tag + "_stat")
                self.aggr = sem(tag + "_aggr")
                self.vars = sem(tag + "_vars")
                self.inv_ready = sem(tag + "_inv_ready")
                self.rstd_ready = sem(tag + "_rstd_ready")
                self.bias_ready = sem(tag + "_bias_ready")
                self.normed = sem(tag + "_normed")
                self.staged = sem(tag + "_staged")

        one, two = Layer("a"), Layer("b")

        block = ctx.enter_context(nc.Block())

        SETUP_LOADS = 14

        @block.sync
        def _(sp):
            for dst, src in (
                (w0_sb[:], w0_t.rearrange("(h p) n -> p h n", p=P)),
                (w1_nat, w1.rearrange("(h p) n -> p h n", p=P)),
                (b0_all[:], b0.partition_broadcast(P)),
                (att_cols[:], att[0:2 * D].rearrange("(c p) -> p c", p=P)),
                (att_edge[:], att[2 * D:2 * D + DE].partition_broadcast(P)),
                (src_idx[:], src_lane), (dst_l[:], dst_lane),
                (l_next, dst_next_lane), (a_dst, dst_rows), (a_prev, dst_prev_rows),
                (a_next, dst_next_rows), (a_up, dst_up_rows), (a_up_next, dst_up_next_rows),
                (code_sb, code_step),
            ):
                sp.dma_start(dst, src, allow_slow_non_contiguous=True).then_inc(loaded, DMA)
            sp.wait_ge(leads_ready, 1)
            sp.dma_start(lead_line.rearrange("(h t e) -> t h e", h=2, e=P), lead_f).then_inc(leads_stored, DMA)
            sp.wait_ge(setup_done, 1)
            sp.wait_ge(leads_stored, DMA)

            def load_line(ly, g, s, with_src):
                wait(sp, ly.y_ready, GT * (g - 1))
                sp.dma_start(carries[P - 1:P, s, :], lead_groups[g]).then_inc(ly.line_loaded[s], DMA)
                sp.dma_start(dst_line_sb[:, s, :], dst_groups[g].partition_broadcast(P)).then_inc(ly.line_loaded[s], DMA)
                if with_src:
                    sp.dma_start(src_line_sb[:, s, :], src_groups[g].partition_broadcast(HT)).then_inc(ly.line_loaded[s], DMA)

            def half_of(a, s, half):
                return a[:, s, half * HB:(half + 1) * HB].rearrange("p r d -> p (r d)")

            def load_x(g, s, half):
                sp.dma_start(half_of(x_in, s, half), block_of(x_blocks, x, g, half)).then_inc(x_loaded[s], DMA)

            def store_x(g, s, half):
                sp.wait_ge(x_normed, 2 * g + half + 1)
                sp.sem_inc(moves_open, 1)
                if isinstance(g, int) and g == GROUPS - 1 and half == 0:
                    sp.wait_ge(one_stored[1 - s], DMA * GROUPS)
                    sp.wait_ge(two_stored[1 - s], DMA * GROUPS)
                sp.dma_start(block_of(t_blocks, table[0:N, :], g, half), half_of(x_one, s, half)).then_inc(one_stored[s], DMA)
                sp.dma_start(block_of(o_blocks, out, g, half), half_of(x_two, s, half)).then_inc(two_stored[s], DMA)

            def store_rep(g, s):
                sp.wait_ge(one.normed, g + 1)
                sp.dma_start(rep_blocks[g], dst_rows_sb[:, s].rearrange("p k d -> p (k d)")).then_inc(one.stored[s], DMA)

            def move_one(g, s, it):
                if is_group(g + 2):
                    load_line(one, g + 2, s, True)
                if is_group(g - 1):
                    store_x(g - 1, 1 - s, 1)
                if is_group(g + 1):
                    load_x(g + 1, 1 - s, 1)
                if is_group(g - 1):
                    store_rep(g - 1, 1 - s)
                store_x(g, s, 0)
                if is_group(g + 2):
                    load_x(g + 2, s, 0)

            for s in range(2):
                load_line(one, s, s, True)
                load_x(s, s, 0)
            load_x(0, 0, 1)
            every_group(sp, move_one, 4)
            store_x(GROUPS - 1, 1, 1)
            store_rep(GROUPS - 1, 1)

            for s in range(2):
                sp.wait_ge(one_stored[s], DMA * GROUPS)
                sp.wait_ge(two_stored[s], DMA * GROUPS)
            sp.dma_start(w1_sb, w1_t.rearrange("(h p) n -> p h n", p=P)).then_inc(loaded, DMA)

            def attr_and_keep(g, s, it):
                wait(sp, logit_done, g - 1)
                sp.dma_start(attr_sb[:, s, :], attr_groups[g]).then_inc(attr_loaded[s], DMA)
                keep(g - 1, 1 - s)

            def keep(g, s):
                if is_group(g):
                    sp.wait_ge(row_projected, GT * (g + 1))
                    sp.dma_start(by_edge[g], proj[:, s * GT:(s + 1) * GT].rearrange("p k d -> p (k d)")).then_inc(row_kept[s], DMA)

            every_group(sp, attr_and_keep)
            keep(GROUPS - 1, 1)

            def load_two(g, s, it):
                load_line(two, g, s, False)
                wait(sp, two.y_ready, GT * (g - 1))
                sp.dma_start(src_rows_sb[:, s].rearrange("p k d -> p (k d)"), by_edge[g]).then_inc(two.src_loaded[s], DMA)
                wait(sp, two.summed, g - 1)
                sp.dma_start(dst_rows_sb[:, s].rearrange("p k d -> p (k d)"), rep_blocks[g]).then_inc(two.dst_loaded[s], DMA)

            for s in range(2):
                sp.wait_ge(row_kept[s], DMA * GROUPS // 2)
                sp.wait_ge(one.stored[s], DMA * GROUPS // 2)
            sp.wait_ge(row_dotted, GROUPS)
            every_group(sp, load_two)

        @block.gpsimd
        def _(pool):
            nc.gpsimd.memset(ident[:], 0.0).then_inc(consts_ready, 1)
            nc.gpsimd.memset(dst_rows_sb[:], 0.0).then_inc(consts_ready, 1)
            nc.gpsimd.memset(zeros_r, 0.0).then_inc(consts_ready, 1)
            nc.gpsimd.memset(ones_r, 1.0).then_inc(consts_ready, 1)
            nc.gpsimd.iota(lane_code[:], [[GT, P]], base=1, channel_multiplier=0,
                           allow_small_or_imprecise_dtypes=True).then_inc(consts_ready, 1)
            pool.wait_ge(consts_ready, 5)
            nc.gpsimd.affine_select(out=ident[:], in_=ident[:], compare_op=ALU.not_equal, fill=1.0,
                                    base=0, pattern=[[-1, P]], channel_multiplier=1).then_inc(consts_ready, 1)
            nc.gpsimd.memset(carried[:], 0.0).then_inc(consts_ready, 1)
            nc.gpsimd.memset(carries[:], 0.0).then_inc(consts_ready, 1)
            pool.wait_ge(setup_done, 1)

            def gather(dst, src, idx, k, bound, done_sem):
                pool.indirect_dma_start(
                    out=dst, out_offset=None, in_=src,
                    in_offset=bass.IndirectOffsetOnAxis(ap=idx[:, k:k + 1], axis=0),
                    bounds_check=bound, oob_is_err=False).then_inc(done_sem, DMA)

            def gather_src(g, s, it):
                wait(pool, one.src_loaded[s], GT * DMA * it)
                nc.gpsimd.tensor_copy(idx_now[:, s, 0, :], src_idx[:, bass.ds(g * GT, GT)]).then_inc(src_staged, 1)
                wait(pool, one.t_ready, GT * (g - 1))
                pool.wait_ge(src_staged, g + 1)
                pool.sem_inc(gathers_open, 1)
                for k in range(GT):
                    gather(src_rows_sb[:, s, k, :], x, idx_now[:, s, 0], k, N - 1, one.src_loaded[s])

            def gather_dst(g, s, it):
                wait(pool, one.dst_loaded[s], GT * DMA * it)
                nc.gpsimd.tensor_copy(idx_now[:, s, 1, :], rep_idx[:, bass.ds(g * GT, GT)]).then_inc(one.staged, 1)
                wait(pool, one.stored[s], DMA * it)
                pool.wait_ge(one.staged, g + 1)
                pool.sem_inc(gathers_open, 1)
                for k in range(GT):
                    gather(dst_rows_sb[:, s, k, :], x, idx_now[:, s, 1], k, N - 1, one.dst_loaded[s])

            def gathers_one(g, s, it):
                if is_group(g + 1):
                    gather_src(g + 1, 1 - s, it + s)
                gather_dst(g, s, it)

            gather_src(0, 0, 0)
            every_group(pool, gathers_one)

            for s in range(2):
                pool.wait_ge(one_stored[s], DMA * GROUPS)
                pool.wait_ge(one.stored[s], DMA * GROUPS // 2)
            pool.wait_ge(match_done, GROUPS + 1)

            def gather_row(g, s, it):
                wait(pool, row_loaded[s], GT * DMA * it)
                nc.gpsimd.tensor_copy(idx_now[:, s, 0, :], row_idx[:, bass.ds(g * GT, GT)]).then_inc(row_staged, 1)
                pool.wait_ge(row_staged, g + 1)
                wait(pool, row_dotted, g - 1)
                pool.sem_inc(gathers_open, 1)
                for k in range(GT):
                    wait(pool, row_turned, GT * (g - 2) + k + 1)
                    pool.sem_inc(gathers_open, 1)
                    gather(src_rows_sb[:, s, k, :], table, idx_now[:, s, 0], k, N + EPAD - 1, row_loaded[s])

            pool.wait_ge(one.t_ready, TILES)
            for s in range(2):
                pool.wait_ge(one.src_loaded[s], GT * DMA * GROUPS // 2)
                pool.wait_ge(one.dst_loaded[s], GT * DMA * GROUPS // 2)
            every_group(pool, gather_row)

            for s in range(2):
                pool.wait_ge(two_stored[s], DMA * GROUPS)
                pool.wait_ge(row_loaded[s], GT * DMA * GROUPS // 2)

            def scatter(g, s, it):
                wait(pool, two.stored[s], GT * DMA * it)
                nc.gpsimd.tensor_copy(idx_now[:, s, 1, :], rep_idx[:, bass.ds(g * GT, GT)]).then_inc(two.staged, 1)
                pool.wait_ge(two.staged, g + 1)
                pool.wait_ge(two.normed, GT * (g + 1))
                pool.sem_inc(gathers_open, 1)
                for k in range(GT):
                    pool.indirect_dma_start(
                        out=out, out_offset=bass.IndirectOffsetOnAxis(ap=idx_now[:, s, 1, k:k + 1], axis=0),
                        in_=finished[:, s * GT + k, :], in_offset=None,
                        bounds_check=N - 1, oob_is_err=False).then_inc(two.stored[s], DMA)

            every_group(pool, scatter)
            for s in range(2):
                pool.wait_ge(two.stored[s], GT * DMA * GROUPS // 2)

        @block.tensor
        def _(pe):
            pe.wait_ge(wide_ready, 1)
            for j in range(2):
                for h in range(HALVES):
                    last = nc.tensor.matmul(ps_y[:, j, 0:D], att_wide[:, 2 * j + h, :], w1_nat[:, h, :],
                                            start=h == 0, stop=h == HALVES - 1)
            last.then_inc(u_ready, 1)

            def scan_turns(n, row, tail):
                pe.wait_ge(tails_ready, n + 1)
                for h in range(2):
                    last = nc.tensor.transpose(ps_m[0:1, h * HT:(h + 1) * HT], row[:, h, tail:tail + 1], ident[0:HT, 0:HT])
                last.then_inc(tails_row, 1)
                off = 0 if tail else 1
                pe.wait_ge(chain_ready, n + 1)
                for h in range(2):
                    last = nc.tensor.transpose(ps_m[0:HT, 256 + h:257 + h], chain_row[:, off + h * HT:off + (h + 1) * HT],
                                               ident[0:1, 0:1])
                last.then_inc(chain_cols, 1)

            def to_lanes(n, row):
                pe.wait_ge(flip_ready, n + 1)
                for h in range(2):
                    last = nc.tensor.transpose(ps_m[:, h * HT:(h + 1) * HT], row[:, h, :], ident[0:HT, 0:HT])
                last.then_inc(flipped, 1)

            def to_rows(n, lanes):
                pe.wait_ge(flip_ready, n + 1)
                for h in range(2):
                    last = nc.tensor.transpose(ps_m[0:HT, h * P:(h + 1) * P], lanes[:, h * HT:(h + 1) * HT], ident[:])
                last.then_inc(flipped, 1)

            def wholes_to_row(n):
                pe.wait_ge(flip_ready, n + 1)
                for j, (row, tail) in enumerate(((lead_f, P - 1), (lead_r, 0))):
                    for h in range(2):
                        last = nc.tensor.transpose(ps_m[0:1, j * TILES + h * HT:j * TILES + (h + 1) * HT],
                                                   row[:, h, tail:tail + 1], ident[0:HT, 0:HT])
                last.then_inc(flipped, 1)

            wholes_to_row(0)
            scan_turns(0, r_a, P - 1)
            to_lanes(1, r_f)

            def search(g, s):
                pe.wait_ge(one.select_ready, g + 1)
                wait(pe, match_done, g)
                for k in range(GT):
                    into = ps_d[:, k // 3, k % 3 * CODE:(k % 3 + 1) * CODE]
                    for n, (h, step) in enumerate(((0, step_hi), (0, step_lo), (1, step_hi), (1, step_lo))):
                        last = nc.tensor.matmul(into, below[:, h, s, k * P:(k + 1) * P], step[:, h, :],
                                                start=n == 0, stop=n == 3)
                last.then_inc(search_ready, 1)

            def slot_of(s, k):
                return (GT * s + k) % 2

            def project(g, s, k, w, t_copied, y_copied, stop):
                slot = slot_of(s, k)
                pe.wait_ge(t_copied, GT * g + k + 1)
                wait(pe, y_copied, GT * g + k - 1)
                for h in range(HALVES):
                    last = nc.tensor.matmul(ps_y[:, slot, 0:D], sums_t[:, slot, h * P:(h + 1) * P], w[:, h, :],
                                            start=h == 0, stop=stop and h == HALVES - 1)
                return last

            def add_one(g, s, it):
                search(g, s)
                pe.wait_ge(one.src_loaded[s], GT * DMA * (it + 1))

                def sums(k):
                    wait(pe, one.t_copied, GT * g + k - 1)
                    for h in range(HALVES):
                        last = nc.tensor.matmul(ps_t[:, slot_of(s, k), h * P:(h + 1) * P],
                                                src_rows_sb[:, s, k, h * P:(h + 1) * P],
                                                same[:, s, k * P:(k + 1) * P], start=True, stop=True)
                    last.then_inc(one.t_ready, 1)

                def finish(k):
                    slot = slot_of(s, k)
                    project(g, s, k, w0_sb, one.t_copied, one.y_copied, False)
                    nc.tensor.matmul(ps_y[:, slot, 0:D], same[:, s, k * P:(k + 1) * P], b0_all[:], start=False, stop=False)
                    wait(pe, one.y_copied, GT * g + k)
                    nc.tensor.matmul(ps_y[:, slot, 0:D], carries[:, s, k * P:(k + 1) * P], carried[:, 1 - slot, :],
                                     start=False, stop=True).then_inc(one.y_ready, 1)

                sums(0)
                for k in range(1, GT):
                    sums(k)
                    finish(k - 1)
                finish(GT - 1)

            every_group(pe, add_one)

            def rows_of(g, s, it):
                pe.wait_ge(row_loaded[s], GT * DMA * (it + 1))

                def turn(k):
                    wait(pe, row_turn_copied, GT * g + k - 1)
                    for h in range(HALVES):
                        last = nc.tensor.transpose(ps_t[:, slot_of(s, k), h * P:(h + 1) * P],
                                                   src_rows_sb[:, s, k, h * P:(h + 1) * P], ident[:])
                    last.then_inc(row_turned, 1)

                def finish(k):
                    project(g, s, k, w1_sb, row_turn_copied, row_projected, True).then_inc(row_projecting, 1)

                turn(0)
                for k in range(1, GT):
                    turn(k)
                    finish(k - 1)
                finish(GT - 1)

            pe.wait_ge(one.y_copied, TILES)
            pe.wait_ge(loaded, (SETUP_LOADS + 1) * DMA)
            every_group(pe, rows_of)

            wholes_to_row(2)
            to_rows(3, l_a)
            scan_turns(1, r_b, 0)
            to_rows(4, l_b)
            scan_turns(2, r_d, P - 1)
            scan_turns(3, r_e, 0)
            scan_turns(4, r_f, P - 1)
            to_lanes(5, r_a)
            to_lanes(6, r_b)

            def add_two(g, s, it):
                pe.wait_ge(two.select_ready, g + 1)
                pe.wait_ge(two.src_loaded[s], DMA * (it + 1))
                for k in range(GT):
                    slot = slot_of(s, k)
                    very_first = isinstance(g, int) and g == 0 and k == 0
                    wait(pe, two.y_copied, GT * g + k - 1)
                    last = nc.tensor.matmul(ps_y[:, slot, 0:D], same[:, s, k * P:(k + 1) * P], src_rows_sb[:, s, k, :],
                                            start=True, stop=very_first)
                    if not very_first:
                        pe.wait_ge(two.y_copied, GT * g + k)
                        before = proj[:, s * GT + k - 1, :] if k else carried[:, 0, :]
                        last = nc.tensor.matmul(ps_y[:, slot, 0:D], carries[:, s, k * P:(k + 1) * P], before,
                                                start=False, stop=True)
                    last.then_inc(two.y_ready, 1)

            every_group(pe, add_two)

        @block.scalar
        def _(act):
            def slot_of(s, k):
                return (GT * s + k) % 2

            def copies_one(g, s, k):
                if k < GT:
                    act.wait_ge(one.t_ready, GT * g + k + 1)
                    nc.scalar.copy(sums_t[:, slot_of(s, k), :], ps_t[:, slot_of(s, k), 0:D]).then_inc(one.t_copied, 1)
                if k:
                    slot = slot_of(s, k - 1)
                    act.wait_ge(one.y_ready, GT * g + k)
                    if k == 1:
                        wait(act, one.normed, g - 1)
                    nc.scalar.activation(proj[:, GT * s + k - 1, :], ps_y[:, slot, 0:D], ACT.Relu)
                    nc.scalar.copy(carried[:, slot, :], ps_y[:, slot, 0:D]).then_inc(one.y_copied, 1)

            def node_rstd(g):
                wait(act, x_normed, 2 * g)
                act.wait_ge(n_inv_ready, g + 1)
                nc.scalar.activation(n_rstd[:], n_inv[:], ACT.Sqrt).then_inc(n_rstd_ready, 1)

            def node_norm(g, s, it, r):
                if r == 0:
                    act.wait_ge(n_bias_ready, g + 1)
                    wait(act, one_stored[s], 2 * DMA * it)
                    wait(act, two_stored[s], 2 * DMA * it)
                nc.scalar.activation(x_one[:, s, r, :], x_in[:, s, r, :], ACT.Identity,
                                     bias=n_bias[:, 0, r:r + 1], scale=n_rstd[:, 0, r:r + 1])
                last = nc.scalar.activation(x_two[:, s, r, :], x_in[:, s, r, :], ACT.Identity,
                                            bias=n_bias[:, 1, r:r + 1], scale=n_rstd[:, 1, r:r + 1])
                if r % HB == HB - 1:
                    last.then_inc(x_normed, 1)

            def edge_rstd(ly, g, each):
                wait(act, ly.normed, each * g)
                act.wait_ge(ly.inv_ready, g + 1)
                nc.scalar.activation(e_rstd[:], e_inv[:], ACT.Sqrt).then_inc(ly.rstd_ready, 1)

            def edge_norm(g, s):
                act.wait_ge(one.bias_ready, g + 1)
                for k in range(GT):
                    last = nc.scalar.activation(dst_rows_sb[:, s, k, :], proj[:, GT * s + k, :], ACT.Identity,
                                                bias=e_bias[:, k:k + 1], scale=e_rstd[:, k:k + 1])
                last.then_inc(one.normed, 1)

            def turn_one(g, s, it):
                node_rstd(g)
                if is_group(g - 1):
                    edge_norm(g - 1, 1 - s)
                for k in range(GT):
                    if is_group(g + 1):
                        copies_one(g + 1, 1 - s, k)
                    node_norm(g, s, it, 2 * k)
                    node_norm(g, s, it, 2 * k + 1)
                if is_group(g + 1):
                    copies_one(g + 1, 1 - s, GT)
                edge_rstd(one, g, 1)

            act.wait_ge(setup_done, 1)
            for k in range(GT + 1):
                copies_one(0, 0, k)
            every_group(act, turn_one)
            edge_norm(GROUPS - 1, 1)

            def copies_rows(g, s, it):
                for k in range(GT + 1):
                    if k < GT:
                        act.wait_ge(row_turned, GT * g + k + 1)
                        nc.scalar.copy(sums_t[:, slot_of(s, k), :], ps_t[:, slot_of(s, k), 0:D]).then_inc(row_turn_copied, 1)
                    if k:
                        act.wait_ge(row_projecting, GT * g + k)
                        if k == 1:
                            wait(act, row_kept[s], DMA * it)
                        nc.scalar.copy(proj[:, GT * s + k - 1, :], ps_y[:, slot_of(s, k - 1), 0:D]).then_inc(row_projected, 1)

            every_group(act, copies_rows)

            act.wait_ge(exp_ready, 1)
            nc.scalar.activation(r_e, r_e, ACT.Exp).then_inc(exp_done, 1)

            for s in range(2):
                act.wait_ge(one.stored[s], DMA * GROUPS // 2)
                act.wait_ge(row_kept[s], DMA * GROUPS // 2)

            def copy_two(g, s, k):
                wait(act, two.normed, GT * (g - 2) + k + 1)
                act.wait_ge(two.y_ready, GT * g + k + 1)
                last = nc.scalar.copy(proj[:, GT * s + k, :], ps_y[:, slot_of(s, k), 0:D])
                if k == GT - 1:
                    last = nc.scalar.copy(carried[:, 0, :], ps_y[:, slot_of(s, k), 0:D])
                last.then_inc(two.y_copied, 1)

            def norm_two(g, s, k):
                if k == 0:
                    act.wait_ge(two.bias_ready, g + 1)
                nc.scalar.activation(finished[:, s * GT + k, :], proj[:, GT * s + k, :], ACT.Identity,
                                     bias=e_bias[:, k:k + 1], scale=e_rstd[:, k:k + 1]).then_inc(two.normed, 1)

            def turn_two(g, s, it):
                for k in range(GT + 1):
                    if k < GT and is_group(g - 1):
                        norm_two(g - 1, 1 - s, k)
                    if k and is_group(g + 1):
                        copy_two(g + 1, 1 - s, k - 1)
                edge_rstd(two, g, GT)
                wait(act, two.stored[s], GT * DMA * it)

            for k in range(GT):
                copy_two(0, 0, k)
            every_group(act, turn_two)
            for k in range(GT):
                norm_two(GROUPS - 1, 1, k)

        @block.vector
        def _(dve):
            v = nc.vector
            steps = [0]

            def link(ins):
                steps[0] += 1
                ins.then_inc(dve_step, 1)
                dve.wait_ge(dve_step, steps[0])

            def link_all(instructions):
                for ins in instructions:
                    steps[0] += 1
                    ins.then_inc(dve_step, 1)
                dve.wait_ge(dve_step, steps[0])

            def seg_scan(n, vals, into, reverse, biggest):
                flags = (ban_r if reverse else ban_f) if biggest else (keep_r if reverse else keep_f)
                leads = (nolead_r if reverse else nolead_f) if biggest else (lead_r if reverse else lead_f)
                whole_row = whole[:, 2 * biggest + reverse, :]
                start = -BIG if biggest else 0.0
                op0, op1 = (ALU.add, ALU.max) if biggest else (ALU.mult, ALU.add)
                way = slice(None, None, -1) if reverse else slice(None)
                for h in range(2):
                    last = v.tensor_tensor_scan(into[:, h, way], flags[:, h, way], vals[:, h, way], start, op0, op1)
                last.then_inc(tails_ready, 1)
                row = chain_row[:, 0:TILES] if reverse else chain_row[:, 1:TILES + 1]
                link(v.memset(chain_row[:, TILES:TILES + 1] if reverse else chain_row[:, 0:1], start))
                dve.wait_ge(tails_row, n + 1)
                v.tensor_tensor_scan(row[:, way], whole_row[:, way], ps_m[0:1, 0:TILES][:, way], start,
                                     op0, op1).then_inc(chain_ready, 1)
                dve.wait_ge(chain_cols, n + 1)
                link_all(v.scalar_tensor_tensor(into[:, h, :], leads[:, h, :], ps_m[0:HT, 256 + h:257 + h],
                                                into[:, h, :], op0, op1) for h in range(2))

            def copy_wholes(n):
                dve.wait_ge(flipped, n + 1)
                for j in range(2):
                    v.tensor_copy(whole[:, j, :], ps_m[0:1, j * TILES:(j + 1) * TILES])
                link_all(v.tensor_scalar(whole[:, 2 + j, :], ps_m[0:1, j * TILES:(j + 1) * TILES], 1.0, BIG,
                                         ALU.subtract, ALU.mult) for j in range(2))

            dve.wait_ge(loaded, SETUP_LOADS * DMA)
            dve.wait_ge(consts_ready, 8)
            link_all((
                v.tensor_scalar(relu_b0[:], b0_all[:], 0.0, None, ALU.max),
                v.tensor_tensor(keep_f, a_dst, a_prev, ALU.is_equal),
                v.tensor_tensor(keep_r, a_dst, a_next, ALU.is_equal),
                v.tensor_tensor(rep_l[:], dst_l[:], l_next, ALU.not_equal),
                v.tensor_scalar(src_next1[:], src_idx[:], 1.0, None, ALU.add),
                v.tensor_copy(tile_first[:], a_dst[:, :, 0]),
                v.tensor_scalar(r_b, a_dst, 1.0, None, ALU.add),
                v.tensor_scalar(r_c, a_up, 1.0, None, ALU.add),
                v.tensor_tensor(r_d, a_dst, a_next, ALU.not_equal),
                v.tensor_tensor(r_e, a_up, a_up_next, ALU.not_equal),
            ))
            v.tensor_copy(att_wide, att_cols[:].unsqueeze(2).to_broadcast([P, 4, P])).then_inc(wide_ready, 1)
            link_all(v.tensor_tensor_scan(into[:, h, way], keep[:, h, way], zeros_r[:, h, :], 1.0, ALU.mult, ALU.add)
                     for into, keep, way in ((lead_f, keep_f, slice(None)), (lead_r, keep_r, slice(None, None, -1)))
                     for h in range(2))
            v.memset(l_b, 0.0).then_inc(leads_ready, 1)
            dve.wait_ge(leads_ready, 1)
            v.memset(l_b, 0.0).then_inc(flip_ready, 1)
            link_all((v.tensor_tensor(r_b, r_b, r_d, ALU.mult), v.tensor_tensor(r_c, r_c, r_e, ALU.mult)))
            link(v.tensor_tensor(r_b, r_b, r_c, ALU.subtract))
            link(v.tensor_copy(r_int, r_b))
            link(v.tensor_single_scalar(r_int2, r_int, 255, ALU.bitwise_and))
            link(v.tensor_copy(r_c, r_int2))
            link_all((
                v.tensor_tensor(step_hi[:, :, 0:P], r_b, r_c, ALU.subtract),
                v.tensor_copy(step_lo[:, :, 0:P], r_c),
                v.tensor_copy(step_hi[:, :, P], code_sb[:, :, 0]),
                v.tensor_copy(step_lo[:, :, P], code_sb[:, :, 1]),
                v.tensor_scalar(l_a, rep_l[:], -1.0, -float(FAR), ALU.add, ALU.mult),
            ))
            link(v.tensor_tensor(rep_idx[:], l_a, dst_l[:], ALU.add))
            copy_wholes(0)
            seg_scan(0, ones_r, r_a, 0, 0)
            v.tensor_copy(r_f, r_a).then_inc(flip_ready, 1)
            dve.wait_ge(flipped, 2)
            link(v.reciprocal(per_count[:], ps_m[:, 0:TILES]))
            dve.wait_ge(u_ready, 1)
            link_all((v.tensor_copy(u_src[:], ps_y[:, 0, 0:D]), v.tensor_copy(u_dst[:], ps_y[:, 1, 0:D])))
            v.reduce_sum(u_sum[:], u_dst[:], axis=mybir.AxisListType.X).then_inc(setup_done, 1)
            dve.wait_ge(setup_done, 1)

            def cols(a, g):
                return a[:, bass.ds(g * GT, GT)]

            def col(a, g, k):
                return a[:, bass.ds(g * GT + k, 1)]

            def selectors(g, s, it):
                dve.wait_ge(one.line_loaded[s], 3 * DMA * (it + 1))
                wait(dve, one.y_ready, GT * (g - 1))
                wait(dve, search_ready, g - 1)
                v.tensor_tensor(same[:, s, :].rearrange("p (k e) -> p k e", k=GT),
                                dst_line_sb[:, s, :].rearrange("p (k e) -> p k e", k=GT),
                                cols(dst_l, g).unsqueeze(2).to_broadcast([P, GT, P]), ALU.is_equal)
                for h in range(2):
                    last = v.tensor_scalar(below[:, h, s, :], src_line_sb[:, s, :], tile_first[:, h:h + 1], None, ALU.is_ge)
                last.then_inc(one.select_ready, 1)

            def aggregate(stats, twice, gap, sq, part, stat, aggr, g):
                dve.wait_ge(stat, g + 1)
                v.tensor_tensor(twice[:], stats[:, :, 1], stats[:, :, 4], ALU.add)
                v.tensor_tensor(sq[:], stats[:, :, 2], stats[:, :, 5], ALU.add)
                v.tensor_tensor(gap[:], stats[:, :, 1], stats[:, :, 4], ALU.subtract).then_inc(aggr, 1)
                dve.wait_ge(aggr, 3 * g + 1)
                v.scalar_tensor_tensor(gap[:], gap[:], 0.25, gap[:], ALU.mult, ALU.mult).then_inc(aggr, 1)
                dve.wait_ge(aggr, 3 * g + 2)
                v.scalar_tensor_tensor(part[:], sq[:], 1.0 / D, gap[:], ALU.mult, ALU.add).then_inc(aggr, 1)
                dve.wait_ge(aggr, 3 * g + 3)

            def node_stats(g, s, it):
                dve.wait_ge(x_loaded[s], 2 * DMA * (it + 1))
                v.tensor_tensor(x_in[:, s], x_in[:, s], relu_b0[:].unsqueeze(1).to_broadcast([P, RB, D]),
                                ALU.add).then_inc(x_shifted, 1)
                dve.wait_ge(x_shifted, g + 1)
                for r in range(RB):
                    last = v.bn_stats(n_stats[:, r, :], x_in[:, s, r, :])
                last.then_inc(n_stat, 1)
                aggregate(n_stats, n_twice, n_gap, n_sq, n_part, n_stat, n_aggr, g)
                v.tensor_scalar(n_var[:, 0, :], n_part[:], EPS, None, ALU.add)
                v.tensor_scalar(n_var[:, 1, :], n_part[:], 1.0 + EPS, EPS * EPS, ALU.mult, ALU.add).then_inc(n_vars, 1)
                dve.wait_ge(n_vars, g + 1)
                v.reciprocal(n_inv[:], n_var[:]).then_inc(n_inv_ready, 1)

            def node_bias(g):
                dve.wait_ge(n_rstd_ready, g + 1)
                v.scalar_tensor_tensor(n_bias[:], n_twice[:].unsqueeze(1).to_broadcast([P, 2, RB]), -0.5, n_rstd[:],
                                       ALU.mult, ALU.mult).then_inc(n_bias_ready, 1)

            def finish_stats(ly, g, s):
                for k in range(GT):
                    last = v.bn_stats(e_stats[:, k, :], proj[:, s * GT + k, :])
                last.then_inc(ly.stat, 1)
                aggregate(e_stats, e_twice, e_gap, e_sq, e_part, ly.stat, ly.aggr, g)
                v.tensor_scalar(e_var[:], e_part[:], EPS, None, ALU.add).then_inc(ly.vars, 1)
                dve.wait_ge(ly.vars, g + 1)
                v.reciprocal(e_inv[:], e_var[:]).then_inc(ly.inv_ready, 1)

            def finish_bias(ly, g):
                dve.wait_ge(ly.rstd_ready, g + 1)
                v.scalar_tensor_tensor(e_bias[:], e_twice[:], -0.5, e_rstd[:], ALU.mult, ALU.mult).then_inc(ly.bias_ready, 1)

            def finish_one(g, s, it):
                dve.wait_ge(one.y_copied, GT * (g + 1))
                dve.wait_ge(one.dst_loaded[s], GT * DMA * (it + 1))
                for k in range(GT):
                    row = proj[:, s * GT + k, :]
                    last = v.scalar_tensor_tensor(row, row, col(per_count, g, k), dst_rows_sb[:, s, k, :], ALU.mult, ALU.add)
                last.then_inc(one.summed, 1)
                node_bias(g)
                dve.wait_ge(one.summed, g + 1)
                for k in range(GT):
                    v.tensor_tensor_reduce(out=scrap[:, k, :], in0=proj[:, s * GT + k, :], in1=u_dst[:], scale=1.0, scalar=0.0,
                                           op0=ALU.mult, op1=ALU.add, accum_out=e_dot[:, 0, k:k + 1])
                finish_stats(one, g, s)

            def score_one(g):
                dve.wait_ge(one.rstd_ready, g + 1)
                v.tensor_tensor(e_tmp[:], e_dot[:, 0, :], e_rstd[:], ALU.mult)
                finish_bias(one, g)
                dve.wait_ge(one.bias_ready, g + 1)
                v.scalar_tensor_tensor(cols(dst_score, g), e_bias[:], u_sum[:], e_tmp[:], ALU.mult, ALU.add)

            def match(g):
                dve.wait_ge(search_ready, g + 1)
                for k in range(GT):
                    at = k % 3 * CODE
                    v.scalar_tensor_tensor(scrap[:, k, 0:P], ps_d[:, k // 3, at:at + P], col(src_next1, g, k), lane_code[:],
                                           ALU.is_equal, ALU.mult, accum_out=col(match_l, g, k))
                v.tensor_copy(code_l[:, bass.ds(g * GT, 6)].rearrange("p (a b) -> p a b", b=3),
                              ps_d[:, 0:2, 0:3 * CODE].rearrange("p a (b c) -> p a b c", c=CODE)[:, :, :, P])
                v.tensor_copy(col(code_l, g, 6), ps_d[:, 2, P:P + 1]).then_inc(match_done, 1)

            def turn_one(g, s, it):
                if is_group(g + 1):
                    selectors(g + 1, 1 - s, it + s)
                node_stats(g, s, it)
                if is_group(g - 1):
                    score_one(g - 1)
                finish_one(g, s, it)
                if is_group(g + 1):
                    match(g + 1)

            selectors(0, 0, 0)
            match(0)
            every_group(dve, turn_one)

            link_all((v.tensor_scalar(weight_l[:], match_l[:], 0.0, None, ALU.is_gt),
                      v.scalar_tensor_tensor(per_total[:], match_l[:], -1.0, code_l[:], ALU.add, ALU.add)))
            link(v.tensor_tensor(per_total[:], per_total[:], src_idx[:], ALU.subtract))
            link(v.tensor_tensor(per_total[:], per_total[:], weight_l[:], ALU.mult))
            v.tensor_tensor(row_idx[:], per_total[:], src_idx[:], ALU.add).then_inc(match_done, 1)
            score_one(GROUPS - 1)

            def dots(g, s, it):
                dve.wait_ge(attr_loaded[s], DMA * (it + 1))
                attrs = attr_sb[:, s, :].rearrange("p (k f) -> p k f", k=GT)
                v.tensor_tensor(attrs, attrs, att_edge[:].unsqueeze(1).to_broadcast([P, GT, DE]), ALU.mult).then_inc(attr_scaled, 1)
                wait(dve, logit_done, g)
                dve.wait_ge(attr_scaled, g + 1)
                v.reduce_sum(e_tmp[:], attrs, axis=mybir.AxisListType.X)
                dve.wait_ge(row_loaded[s], GT * DMA * (it + 1))
                for k in range(GT):
                    last = v.tensor_tensor_reduce(out=scrap[:, k, :], in0=src_rows_sb[:, s, k, :], in1=u_src[:], scale=1.0,
                                                  scalar=0.0, op0=ALU.mult, op1=ALU.add, accum_out=e_dot[:, s, k:k + 1])
                last.then_inc(row_dotted, 1)
                dve.wait_ge(row_dotted, g + 1)
                v.tensor_tensor(cols(logit_l, g), e_dot[:, s, :], e_tmp[:], ALU.add).then_inc(logit_done, 1)

            every_group(dve, dots)
            dve.wait_ge(logit_done, GROUPS)

            for s in range(2):
                dve.wait_ge(one_stored[s], DMA * GROUPS)
                dve.wait_ge(two_stored[s], DMA * GROUPS)
            link_all([v.tensor_scalar(ban, keep, 1.0, BIG, ALU.subtract, ALU.mult)
                      for ban, keep in ((ban_f, keep_f), (ban_r, keep_r), (nolead_f, lead_f), (nolead_r, lead_r))]
                     + [v.tensor_tensor(l_a, dst_score[:], rep_l[:], ALU.mult), v.tensor_copy(l_b, logit_l[:]),
                        v.tensor_copy(dst_float, dst_l[:])])
            v.memset(r_f, 0.0).then_inc(flip_ready, 1)
            copy_wholes(2)

            def rows_of_ps():
                return ps_m[0:HT, 0:2 * P].rearrange("p (h e) -> p h e", h=2)

            v.memset(r_c, 0.0).then_inc(flip_ready, 1)
            dve.wait_ge(flipped, 4)
            link(v.tensor_copy(r_a, rows_of_ps()))
            seg_scan(1, r_a, r_b, 1, 0)
            v.memset(r_d, 0.0).then_inc(flip_ready, 1)
            dve.wait_ge(flipped, 5)
            link(v.tensor_tensor(r_c, rows_of_ps(), r_b, ALU.add))
            link(v.scalar_tensor_tensor(r_c, r_c, ALPHA, r_c, ALU.mult, ALU.max))
            seg_scan(2, r_c, r_d, 0, 1)
            seg_scan(3, r_c, r_e, 1, 1)
            link(v.tensor_tensor(r_d, r_d, r_e, ALU.max))
            v.tensor_tensor(r_e, r_c, r_d, ALU.subtract).then_inc(exp_ready, 1)
            dve.wait_ge(exp_done, 1)
            seg_scan(4, r_e, r_f, 0, 0)
            v.tensor_copy(r_a, r_e).then_inc(flip_ready, 1)
            dve.wait_ge(flipped, 6)
            link(v.tensor_copy(weight_l[:], ps_m[:, 0:TILES]))
            v.tensor_copy(r_b, r_f).then_inc(flip_ready, 1)
            dve.wait_ge(flipped, 7)
            link(v.scalar_tensor_tensor(per_total[:], ps_m[:, 0:TILES], -1.0, rep_l[:], ALU.add, ALU.mult))
            link(v.tensor_scalar(per_total[:], per_total[:], 1.0, None, ALU.add))
            link(v.reciprocal(per_total[:], per_total[:]))

            def selectors_two(g, s, it):
                dve.wait_ge(two.line_loaded[s], 2 * DMA * (it + 1))
                wait(dve, two.y_ready, GT * (g - 1))
                for k in range(GT):
                    last = v.tensor_scalar(same[:, s, k * P:(k + 1) * P], dst_line_sb[:, s, k * P:(k + 1) * P],
                                           col(dst_float, g, k), col(weight_l, g, k), ALU.is_equal, ALU.mult)
                last.then_inc(two.select_ready, 1)

            def finish_two(g, s, it):
                dve.wait_ge(two.y_copied, GT * (g + 1))
                dve.wait_ge(two.dst_loaded[s], DMA * (it + 1))
                for k in range(GT):
                    row = proj[:, s * GT + k, :]
                    last = v.scalar_tensor_tensor(row, row, col(per_total, g, k), dst_rows_sb[:, s, k, :],
                                                  ALU.mult, ALU.add)
                last.then_inc(two.summed, 1)
                dve.wait_ge(two.summed, g + 1)
                finish_stats(two, g, s)

            def turn_two(g, s, it):
                if is_group(g + 1):
                    selectors_two(g + 1, 1 - s, it + s)
                if is_group(g - 1):
                    finish_bias(two, g - 1)
                finish_two(g, s, it)

            selectors_two(0, 0, 0)
            every_group(dve, turn_two)
            finish_bias(two, GROUPS - 1)


def kernel(x, src, dst, edge_attr_64, L0_gnn_W, L0_gnn_b, L1_gnn_W, L1_gnn_A):
    import concourse.bacc as bacc
    from concourse.bass_utils import run_bass_kernel_spmd

    def padded(a, before, after):
        return np.concatenate([np.asarray(before, np.int32),
                               np.asarray(a, np.int32), np.asarray(after, np.int32)])

    def lanes(line):
        return np.ascontiguousarray(line.reshape(TILES, P).T)

    def rows(line):
        return np.ascontiguousarray(line.reshape(2, HT, P).transpose(1, 0, 2))

    src, dst = np.asarray(src), np.asarray(dst)
    src_line = padded(src, [], [0] * (EPAD - E))
    dst_line = padded(dst, [], [PAD_DST] * (EPAD - E))
    dst_next = np.append(dst_line[1:], np.int32(-1))
    dst_prev = np.insert(dst_line[:-1], 0, np.int32(-1))
    dst_up = np.concatenate([np.full(P, -1, np.int32), dst_line[:-P]])
    dst_up_next = np.concatenate([np.full(P, -1, np.int32), dst_next[:-P]])
    code = N + np.arange(TILES) // GT * GE + np.arange(TILES) % GT
    step = np.diff(code, prepend=0)
    code_step = np.stack([step // 256 * 256, step % 256], -1).astype(np.float32).reshape(2, HT, 2).transpose(1, 0, 2)
    attr = np.concatenate([np.asarray(edge_attr_64), np.zeros((EPAD - E, DE), np.float32)])
    attr_lane = np.ascontiguousarray(attr.reshape(TILES, P, DE).transpose(1, 0, 2))
    w0, w1 = np.asarray(L0_gnn_W), np.asarray(L1_gnn_W)
    arrays = {
        "x": np.asarray(x), "src_lane": lanes(src_line), "src_line": src_line, "dst_line": dst_line,
        "dst_lane": lanes(dst_line), "dst_next_lane": lanes(dst_next),
        "dst_rows": rows(dst_line), "dst_prev_rows": rows(dst_prev), "dst_next_rows": rows(dst_next),
        "dst_up_rows": rows(dst_up), "dst_up_next_rows": rows(dst_up_next),
        "code_step": np.ascontiguousarray(code_step), "attr_lane": attr_lane,
        "w0_t": np.ascontiguousarray(w0.T), "w1_t": np.ascontiguousarray(w1.T), "w1": w1,
        "b0": np.asarray(L0_gnn_b), "att": np.asarray(L1_gnn_A)[0],
    }
    nc = bacc.Bacc("TRN2", target_bir_lowering=False, num_devices=1)
    args = [nc.dram_tensor(name, a.shape, mybir.dt.from_np(a.dtype), kind="ExternalInput").ap()
            for name, a in arrays.items()]
    out = nc.dram_tensor("out", (N, D), F32, kind="ExternalOutput").ap()
    gnn_kernel(nc, *args, out)
    r = run_bass_kernel_spmd(nc, [arrays], core_ids=[0])
    return r.results[0]["out"]
```

```python
from contextlib import ExitStack

import numpy as np

import concourse.bass as bass
from concourse import mybir

F32 = mybir.dt.float32
BF16 = mybir.dt.bfloat16
I32 = mybir.dt.int32
U16 = mybir.dt.uint16
ALU = mybir.AluOpType
ACT = mybir.ActivationFunctionType

P = 128
N, D, E, DE = 50000, 256, 25000, 64
HALVES = D // P
GT = 7
TILES = 196
GROUPS = TILES // GT
GE = GT * P
EPAD = TILES * P
HT = TILES // 2
RB = 14
HB = RB // 2
BLOCK = P * RB
LAST_BLOCK = N - BLOCK
EPS = 1e-5
ALPHA = 0.2
BIG = 1e37
PAD_DST = 65535
FAR = 65536
CODE = P + 1
assert BLOCK * (GROUPS - 1) < N <= BLOCK * GROUPS and GROUPS % 2 == 0 and TILES == GROUPS * GT
DMA = 16


def gnn_kernel(nc, x, src_line, src_lane, dst_framed, dst_lane, dst_next_lane, code_step, attr_lane,
               w0_t, w1_t, w1, b0, att, out):
    table = nc.dram_tensor("row_table", (N + EPAD, D), F32).ap()
    by_edge = nc.dram_tensor("rows_by_edge", (GROUPS, P, GT * D), F32).ap()
    lead_line = nc.dram_tensor("lead_line", (EPAD,), F32).ap()
    x_blocks = x[0:BLOCK * (GROUPS - 1), :].rearrange("(g p r) d -> g p (r d)", p=P, r=RB)
    t_blocks = table[0:BLOCK * (GROUPS - 1), :].rearrange("(g p r) d -> g p (r d)", p=P, r=RB)
    o_blocks = out[0:BLOCK * (GROUPS - 1), :].rearrange("(g p r) d -> g p (r d)", p=P, r=RB)
    rep_blocks = table[N:N + EPAD, :].rearrange("(g p k) d -> g p (k d)", p=P, k=GT)
    src_ordered = nc.dram_tensor("src_ordered", (EPAD, 1), I32).ap()
    dst_ordered = nc.dram_tensor("dst_ordered", (P + EPAD + 1,), I32).ap()
    dst_by_rank = nc.dram_tensor("dst_by_rank", (EPAD, 1), I32).ap()
    attr_ordered = nc.dram_tensor("attr_ordered", (EPAD, DE), F32).ap()
    src_line16 = nc.dram_tensor("src_line16", (EPAD,), U16).ap()
    dst_line16 = nc.dram_tensor("dst_line16", (EPAD,), U16).ap()
    src_groups = src_line16.rearrange("(g e) -> g e", e=GE)
    dst_groups = dst_line16.rearrange("(g e) -> g e", e=GE)
    lead_groups = lead_line.rearrange("(g o e) -> g o e", o=1, e=GE)
    attr_ordered_groups = attr_ordered.rearrange("(g k p) f -> g p k f", k=GT, p=P)
    attr_groups = attr_lane.rearrange("p (g k) f -> g p (k f)", k=GT)

    def block_of(blocks, whole, g, half):
        if isinstance(g, int) and g == GROUPS - 1:
            return whole[LAST_BLOCK:N, :].rearrange("(p r) d -> p (r d)", r=RB)[:, half * HB * D:(half + 1) * HB * D]
        return blocks[g][:, half * HB * D:(half + 1) * HB * D]

    def is_group(g):
        return not isinstance(g, int) or 0 <= g < GROUPS

    def wait(engine, semaphore, count):
        if not isinstance(count, int) or count > 0:
            engine.wait_ge(semaphore, count)

    def every_group(engine, turn, apart=2):
        for g in (0, 1):
            turn(g, g, 0)
        with engine.Fori(1, (GROUPS - apart) // 2) as i:
            for s in range(2):
                turn(2 * i + s, s, i)
        for g in range(GROUPS - apart, GROUPS):
            turn(g, g % 2, g // 2)

    ctx = ExitStack()
    with ctx:
        def sb(name, shape, dt=F32):
            return ctx.enter_context(nc.sbuf_tensor(name, shape, dt))

        def ps(name, shape, dt=F32):
            return ctx.enter_context(nc.psum_tensor(name, shape, dt))

        def sem(name):
            return ctx.enter_context(nc.semaphore(name))

        def pair(name):
            return [sem(f"{name}{s}") for s in range(2)]

        w0_sb = sb("w0_sb", [P, HALVES, D])
        b0_all = sb("b0_all", [P, D])
        relu_b0 = sb("relu_b0", [P, D])
        u_src = sb("u_src", [P, D])
        u_dst = sb("u_dst", [P, D])
        u_sum = sb("u_sum", [P, 1])
        ident = sb("ident", [P, P])
        lane_code = sb("lane_code", [P, P])
        att_cols = sb("att_cols", [P, 4])
        att_edge = sb("att_edge", [P, DE])
        src_idx = sb("src_idx", [P, TILES], I32)
        rep_idx = sb("rep_idx", [P, TILES], I32)
        row_idx = sb("row_idx", [P, TILES], I32)
        dst_l = sb("dst_l", [P, TILES], I32)
        src_next1 = sb("src_next1", [P, TILES])
        rep_l = sb("rep_l", [P, TILES])
        per_count = sb("per_count", [P, TILES])
        match_l = sb("match_l", [P, TILES])
        code_l = sb("code_l", [P, TILES])
        dst_score = sb("dst_score", [P, TILES])
        logit_l = sb("logit_l", [P, TILES])
        weight_l = sb("weight_l", [P, TILES])
        per_total = sb("per_total", [P, TILES])
        src_rows_sb = sb("src_rows_sb", [P, 2, GT, D])
        dst_rows_sb = sb("dst_rows_sb", [P, 2, GT, D])
        dst_line_sb = sb("dst_line_sb", [P, 2, GE], U16)
        src_line_sb = sb("src_line_sb", [HT, 2, GE], U16)
        same = sb("same", [P, 2, GE])
        carries = sb("carries", [P, 2, GE])
        below = sb("below", [HT, 2, 2, GE], BF16)
        sums_t = sb("sums_t", [P, 2, D])
        proj = sb("proj", [P, 2 * GT, D])
        carried = sb("carried", [P, 2, D])
        scrap = sb("scrap", [P, GT, D], BF16)
        idx_now = sb("idx_now", [P, 2, 2, GT], I32)
        e_stats = sb("e_stats", [P, GT, 6])
        e_twice = sb("e_twice", [P, GT])
        e_gap = sb("e_gap", [P, GT])
        e_sq = sb("e_sq", [P, GT])
        e_part = sb("e_part", [P, GT])
        e_var = sb("e_var", [P, GT])
        e_inv = sb("e_inv", [P, GT])
        e_rstd = sb("e_rstd", [P, GT])
        e_bias = sb("e_bias", [P, GT])
        e_dot = sb("e_dot", [P, 2, GT])
        e_tmp = sb("e_tmp", [P, GT])
        disorder_sb = sb("disorder_sb", [1, 1], I32)
        ones_sum = sb("ones_sum", [HT, 1])
        disorder_by = sb("disorder_by", [HT, 1])
        tile_now = sb("tile_now", [P, 3], I32)
        tile_first = sb("tile_first", [HT, 2])
        keep_f, keep_r, lead_f, lead_r = (sb(n, [HT, 2, P])[:] for n in ("keep_f", "keep_r", "lead_f", "lead_r"))
        step_hi = sb("step_hi", [HT, 2, CODE], BF16)
        step_lo = sb("step_lo", [HT, 2, CODE], BF16)
        XB = RB * D
        arena = sb("arena", [P, 6 * XB])
        x_in = arena[:, 0:2 * XB].rearrange("p (s r d) -> p s r d", s=2, r=RB)
        x_one = arena[:, 2 * XB:4 * XB].rearrange("p (s r d) -> p s r d", s=2, r=RB)
        x_two = arena[:, 4 * XB:6 * XB].rearrange("p (s r d) -> p s r d", s=2, r=RB)
        n_stats = sb("n_stats", [P, RB, 6])
        n_twice = sb("n_twice", [P, RB])
        n_gap = sb("n_gap", [P, RB])
        n_sq = sb("n_sq", [P, RB])
        n_part = sb("n_part", [P, RB])
        n_var = sb("n_var", [P, 2, RB])
        n_inv = sb("n_inv", [P, 2, RB])
        n_rstd = sb("n_rstd", [P, 2, RB])
        n_bias = sb("n_bias", [P, 2, RB])

        taken = [2 * XB]

        def view(parts, *shape):
            n = int(np.prod(shape))
            a = arena[0:parts, taken[0]:taken[0] + n]
            taken[0] += n
            if len(shape) == 2:
                a = a.rearrange("p (a b) -> p a b", a=shape[0])
            return a

        def rows(parts=HT):
            return view(parts, 2, P)
        a_dst, a_prev, a_next, a_up, a_up_next, a_src = (rows().bitcast(I32) for _ in range(6))
        dst_u16, src_u16 = (view(HT, P).bitcast(U16).rearrange("p (h e) -> p h e", h=2) for _ in range(2))
        ban_f, ban_r, nolead_f, nolead_r = rows(), rows(), rows(), rows()
        r_a, r_b, r_c, r_d, r_e, r_f = (rows() for _ in range(6))
        zeros_r, ones_r = rows(), rows()
        r_int, r_int2 = rows().bitcast(I32), rows().bitcast(I32)
        code_sb = view(HT, 2, 2)
        whole = view(1, 4, TILES)
        chain_rows = view(1, 2, TILES + 2)
        l_a = view(P, TILES)
        l_next = view(P, TILES).bitcast(I32)
        w1_nat = view(P, HALVES, D)
        w1_sb = view(P, HALVES, D)
        dst_float = view(P, TILES)
        attr_sb = view(P, 2, GT * DE)
        att_wide = view(P, 4, P)
        finished = view(P, 2 * GT, D)
        LINE = HT * P
        half_line = arena[:, 0:LINE]
        half_out = arena[:, LINE:LINE + LINE // 2].bitcast(BF16)
        rank_f = arena[:, LINE + LINE // 2:LINE + LINE // 2 + 3 * TILES].rearrange("p (c t) -> p c t", c=3)
        rank_i = arena[:, LINE + LINE // 2 + 3 * TILES:LINE + LINE // 2 + 4 * TILES].bitcast(I32)
        attr_tile = dst_rows_sb[:, 0, 0, 0:DE]
        before_lane = dst_rows_sb[:, 0, 1, 0:P]

        ps_t = ps("ps_t", [P, 2, 512])
        ps_y = ps("ps_y", [P, 2, 512])
        ps_d = ps("ps_d", [P, 3, 512])
        ps_m = ps("ps_m", [P, 512])
        tail_rows = (ps_m[0:1, 0:TILES], ps_d[0:1, 0, 0:TILES])
        carry_cols = (ps_m[0:HT, 256:258], ps_d[0:HT, 1, 0:2])

        loaded = sem("loaded")
        consts_ready = sem("consts_ready")
        dve_step = sem("dve_step")
        wide_ready = sem("wide_ready")
        u_ready = sem("u_ready")
        tails_ready = sem("tails_ready")
        tails_row = sem("tails_row")
        chain_ready = sem("chain_ready")
        chain_cols = sem("chain_cols")
        flip_ready = sem("flip_ready")
        flipped = sem("flipped")
        exp_ready = sem("exp_ready")
        exp_done = sem("exp_done")
        disorder_counted = sem("disorder_counted")
        disorder_ready = sem("disorder_ready")
        half_loaded = sem("half_loaded")
        half_ranked = sem("half_ranked")
        rank_step = sem("rank_step")
        before_ready = sem("before_ready")
        ranked = sem("ranked")
        attr_tile_loaded = sem("attr_tile_loaded")
        pair_staged = sem("pair_staged")
        moved = sem("moved")
        framed = sem("framed")
        leads_ready = sem("leads_ready")
        lines_stored = sem("lines_stored")
        reloaded = sem("reloaded")
        refilled = sem("refilled")
        setup_done = sem("setup_done")
        src_staged = sem("src_staged")
        gathers_open = sem("gathers_open")
        moves_open = sem("moves_open")
        head_loaded = pair("head_loaded")
        tail_loaded = pair("tail_loaded")
        head_shifted = sem("head_shifted")
        one_stored = pair("one_stored")
        two_stored = pair("two_stored")
        x_shifted, n_stat, n_aggr, n_vars = sem("x_shifted"), sem("n_stat"), sem("n_aggr"), sem("n_vars")
        n_inv_ready, n_rstd_ready, n_bias_ready = sem("n_inv_ready"), sem("n_rstd_ready"), sem("n_bias_ready")
        x_normed = sem("x_normed")
        last_normed = sem("last_normed")
        search_ready, match_done = sem("search_ready"), sem("match_done")
        row_loaded = pair("row_loaded")
        row_kept = pair("row_kept")
        row_staged, row_dotted, logit_done = sem("row_staged"), sem("row_dotted"), sem("logit_done")
        row_turned = sem("row_turned")
        row_turn_copied = sem("row_turn_copied")
        row_projecting = sem("row_projecting")
        row_projected = sem("row_projected")
        attr_loaded = pair("attr_loaded")
        attr_scaled = sem("attr_scaled")

        class Layer:

            def __init__(self, tag):
                self.line_loaded = pair(tag + "_line_loaded")
                self.src_loaded = pair(tag + "_src_loaded")
                self.dst_loaded = pair(tag + "_dst_loaded")
                self.stored = pair(tag + "_stored")
                self.select_ready = sem(tag + "_select_ready")
                self.t_ready = sem(tag + "_t_ready")
                self.t_copied = sem(tag + "_t_copied")
                self.y_ready = sem(tag + "_y_ready")
                self.y_copied = sem(tag + "_y_copied")
                self.summed = sem(tag + "_summed")
                self.stat = sem(tag + "_stat")
                self.aggr = sem(tag + "_aggr")
                self.vars = sem(tag + "_vars")
                self.inv_ready = sem(tag + "_inv_ready")
                self.rstd_ready = sem(tag + "_rstd_ready")
                self.bias_ready = sem(tag + "_bias_ready")
                self.normed = sem(tag + "_normed")
                self.staged = sem(tag + "_staged")

        one, two = Layer("a"), Layer("b")

        def add_bias(on, s, half):
            part = x_in[:, s, half * HB:(half + 1) * HB]
            return on.tensor_tensor(part, part, relu_b0[:].unsqueeze(1).to_broadcast([P, HB, D]), ALU.add)

        block = ctx.enter_context(nc.Block())

        SETUP_LOADS = 15
        RELOADS = 11

        @block.sync
        def _(sp):
            def half_of(a, s, half):
                return a[:, s, half * HB:(half + 1) * HB].rearrange("p r d -> p (r d)")

            def load_x(g, s, half):
                sp.dma_start(half_of(x_in, s, half), block_of(x_blocks, x, g, half)).then_inc(
                    (head_loaded, tail_loaded)[half][s], DMA)

            def load(dst, src, done=loaded):
                sp.dma_start(dst, src, allow_slow_non_contiguous=True).then_inc(done, DMA)

            def rows_from(framed_line, at):
                return framed_line[at:at + EPAD].rearrange("(h t e) -> t h e", h=2, e=P)

            def load_rows(framed_line, done):
                for rows_sb, at in ((a_dst, P), (a_prev, P - 1), (a_next, P + 1), (a_up, 0), (a_up_next, 1)):
                    load(rows_sb, rows_from(framed_line, at), done)

            load_rows(dst_framed, loaded)
            load(a_src, rows_from(src_line, 0))
            for dst, src in (
                (w0_sb[:], w0_t.rearrange("(h p) n -> p h n", p=P)),
                (w1_nat, w1.rearrange("(h p) n -> p h n", p=P)),
                (b0_all[:], b0.partition_broadcast(P)),
                (att_cols[:], att[0:2 * D].rearrange("(c p) -> p c", p=P)),
                (att_edge[:], att[2 * D:2 * D + DE].partition_broadcast(P)),
                (src_idx[:], src_lane), (dst_l[:], dst_lane), (l_next, dst_next_lane), (code_sb, code_step),
            ):
                load(dst, src)

            sp.wait_ge(disorder_ready, 1)
            disorder = sp.value_load(disorder_sb[0:1, 0:1], min_val=0, max_val=EPAD)
            with sp.If(disorder > 0):
                sp.wait_ge(loaded, SETUP_LOADS * DMA)
                for h in range(2):
                    if h:
                        sp.wait_ge(half_ranked, h)
                    load(half_line.bitcast(I32), dst_framed[P + h * LINE:P + (h + 1) * LINE].partition_broadcast(P),
                         half_loaded)
                sp.wait_ge(before_ready, 2)
                load(attr_tile, attr_lane[:, 0, :], attr_tile_loaded)
                with sp.Fori(1, TILES) as t:
                    sp.wait_ge(moved, 3 * DMA * t)
                    sp.dma_start(attr_tile, attr_lane[:, bass.ds(t, 1), :].rearrange("p t f -> p (t f)")).then_inc(
                        attr_tile_loaded, DMA)
                sp.wait_ge(moved, 3 * DMA * TILES)
                load(dst_ordered[0:P], dst_framed[0:P], framed)
                load(dst_ordered[P:P + EPAD], dst_by_rank.rearrange("e o -> (e o)"), framed)
                load(dst_ordered[P + EPAD:P + EPAD + 1], dst_framed[P + EPAD:P + EPAD + 1], framed)
                sp.wait_ge(framed, 3 * DMA)
                load_rows(dst_ordered, reloaded)
                load(a_src, rows_from(src_ordered.rearrange("e o -> (e o)"), 0), reloaded)
                load(w1_nat, w1.rearrange("(h p) n -> p h n", p=P), reloaded)
                load(code_sb, code_step, reloaded)
                load(src_idx[:], src_ordered.rearrange("(t p) o -> p (t o)", p=P), reloaded)
                load(dst_l[:], dst_ordered[P:P + EPAD].rearrange("(t p) -> p t", p=P), reloaded)
                load(l_next, dst_ordered[P + 1:P + 1 + EPAD].rearrange("(t p) -> p t", p=P), reloaded)
            for s in range(2):
                load_x(s, s, 0)
            load_x(0, 0, 1)
            sp.wait_ge(leads_ready, 1)
            for line, rows_sb in ((lead_line, lead_f), (dst_line16, dst_u16), (src_line16, src_u16)):
                sp.dma_start(line.rearrange("(h t e) -> t h e", h=2, e=P), rows_sb).then_inc(lines_stored, DMA)

            def load_line(ly, g, s, with_src):
                wait(sp, ly.y_ready, GT * (g - 1))
                sp.dma_start(carries[P - 1:P, s, :], lead_groups[g]).then_inc(ly.line_loaded[s], DMA)
                sp.dma_start(dst_line_sb[:, s, :], dst_groups[g].partition_broadcast(P)).then_inc(ly.line_loaded[s], DMA)
                if with_src:
                    sp.dma_start(src_line_sb[:, s, :], src_groups[g].partition_broadcast(HT)).then_inc(ly.line_loaded[s], DMA)

            def store_one(g, s, half):
                sp.dma_start(block_of(t_blocks, table[0:N, :], g, half), half_of(x_one, s, half)).then_inc(
                    one_stored[s], DMA)

            def store_two(g, s, half):
                sp.dma_start(block_of(o_blocks, out, g, half), half_of(x_two, s, half)).then_inc(
                    two_stored[s], DMA)

            def store_x(g, s, half):
                if half:
                    sp.wait_ge(last_normed, g + 1)
                    sp.sem_inc(moves_open, 1)
                sp.wait_ge(x_normed, 2 * g + half + 1)
                sp.sem_inc(moves_open, 1)
                store_one(g, s, half)
                store_two(g, s, half)

            def store_rep(g, s):
                sp.wait_ge(one.normed, g + 1)
                sp.dma_start(rep_blocks[g], dst_rows_sb[:, s].rearrange("p k d -> p (k d)")).then_inc(one.stored[s], DMA)

            def move_one(g, s, it):
                if is_group(g + 2):
                    load_line(one, g + 2, s, True)
                if is_group(g - 1):
                    store_x(g - 1, 1 - s, 1)
                if is_group(g + 1):
                    load_x(g + 1, 1 - s, 1)
                if is_group(g - 1):
                    store_rep(g - 1, 1 - s)
                if is_group(g + 1):
                    store_x(g, s, 0)
                if is_group(g + 2):
                    load_x(g + 2, s, 0)

            sp.wait_ge(lines_stored, 3 * DMA)
            for s in range(2):
                load_line(one, s, s, True)
            every_group(sp, move_one, 4)
            sp.wait_ge(x_normed, 2 * GROUPS - 1)
            sp.wait_ge(one_stored[0], DMA * GROUPS)
            store_one(GROUPS - 1, 1, 0)
            sp.wait_ge(last_normed, GROUPS)
            store_one(GROUPS - 1, 1, 1)
            store_rep(GROUPS - 1, 1)
            sp.wait_ge(two_stored[0], DMA * GROUPS)
            for half in range(2):
                store_two(GROUPS - 1, 1, half)

            for s in range(2):
                sp.wait_ge(one_stored[s], DMA * GROUPS)
                sp.wait_ge(two_stored[s], DMA * GROUPS)
            sp.dma_start(w1_sb, w1_t.rearrange("(h p) n -> p h n", p=P)).then_inc(loaded, DMA)

            def attr_and_keep(ordered):
                def turn(g, s, it):
                    wait(sp, logit_done, g - 1)
                    if ordered:
                        sp.dma_start(attr_sb[:, s, :].rearrange("p (k f) -> p k f", k=GT),
                                     attr_ordered_groups[g]).then_inc(attr_loaded[s], DMA)
                    else:
                        sp.dma_start(attr_sb[:, s, :], attr_groups[g]).then_inc(attr_loaded[s], DMA)
                    keep(g - 1, 1 - s)
                return turn

            def keep(g, s):
                if is_group(g):
                    sp.wait_ge(row_projected, GT * (g + 1))
                    sp.dma_start(by_edge[g], proj[:, s * GT:(s + 1) * GT].rearrange("p k d -> p (k d)")).then_inc(row_kept[s], DMA)

            with sp.If(disorder > 0):
                every_group(sp, attr_and_keep(True))
            with sp.Else():
                every_group(sp, attr_and_keep(False))
            keep(GROUPS - 1, 1)

            def load_two(g, s, it):
                load_line(two, g, s, False)
                wait(sp, two.y_ready, GT * (g - 1))
                sp.dma_start(src_rows_sb[:, s].rearrange("p k d -> p (k d)"), by_edge[g]).then_inc(two.src_loaded[s], DMA)
                wait(sp, two.summed, g - 1)
                sp.dma_start(dst_rows_sb[:, s].rearrange("p k d -> p (k d)"), rep_blocks[g]).then_inc(two.dst_loaded[s], DMA)

            for s in range(2):
                sp.wait_ge(row_kept[s], DMA * GROUPS // 2)
                sp.wait_ge(one.stored[s], DMA * GROUPS // 2)
            sp.wait_ge(row_dotted, GROUPS)
            every_group(sp, load_two)

        @block.gpsimd
        def _(pool):
            nc.gpsimd.memset(ident[:], 0.0).then_inc(consts_ready, 1)
            nc.gpsimd.memset(dst_rows_sb[:], 0.0).then_inc(consts_ready, 1)
            nc.gpsimd.memset(zeros_r, 0.0).then_inc(consts_ready, 1)
            nc.gpsimd.memset(ones_r, 1.0).then_inc(consts_ready, 1)
            nc.gpsimd.iota(lane_code[:], [[GT, P]], base=1, channel_multiplier=0,
                           allow_small_or_imprecise_dtypes=True).then_inc(consts_ready, 1)
            pool.wait_ge(consts_ready, 5)
            nc.gpsimd.affine_select(out=ident[:], in_=ident[:], compare_op=ALU.not_equal, fill=1.0,
                                    base=0, pattern=[[-1, P]], channel_multiplier=1).then_inc(consts_ready, 1)
            nc.gpsimd.memset(carried[:], 0.0).then_inc(consts_ready, 1)
            nc.gpsimd.memset(carries[:], 0.0).then_inc(consts_ready, 1)
            pool.wait_ge(disorder_ready, 1)
            pool_disorder = pool.value_load(disorder_sb[0:1, 0:1], min_val=0, max_val=EPAD)
            with pool.If(pool_disorder > 0):
                pool.wait_ge(loaded, SETUP_LOADS * DMA)
                nc.gpsimd.memset(before_lane, 1.0).then_inc(before_ready, 1)
                pool.wait_ge(before_ready, 1)
                nc.gpsimd.affine_select(out=before_lane, in_=before_lane, compare_op=ALU.is_gt, fill=0.0,
                                        base=0, pattern=[[-1, P]], channel_multiplier=1).then_inc(before_ready, 1)
                pool.wait_ge(ranked, 1)
                pool.sem_inc(gathers_open, 1)
                with pool.Fori(1, TILES + 1) as n:
                    for c, what in enumerate((rank_i, src_idx, dst_l)):
                        nc.gpsimd.tensor_copy(tile_now[:, c:c + 1], what[:, bass.ds(n - 1, 1)]).then_inc(pair_staged, 1)
                    pool.wait_ge(pair_staged, 3 * n)
                    pool.sem_inc(gathers_open, 1)
                    pool.wait_ge(attr_tile_loaded, DMA * n)
                    pool.sem_inc(gathers_open, 1)
                    for into, rows_in in ((src_ordered, tile_now[:, 1:2]), (dst_by_rank, tile_now[:, 2:3]),
                                          (attr_ordered, attr_tile)):
                        pool.indirect_dma_start(
                            out=into, out_offset=bass.IndirectOffsetOnAxis(ap=tile_now[:, 0:1], axis=0),
                            in_=rows_in, in_offset=None, bounds_check=EPAD - 1, oob_is_err=False).then_inc(moved, DMA)
                    pool.wait_ge(moved, 3 * DMA * n)
                    pool.sem_inc(gathers_open, 1)
                nc.gpsimd.memset(zeros_r, 0.0).then_inc(refilled, 1)
                nc.gpsimd.memset(ones_r, 1.0).then_inc(refilled, 1)
                pool.wait_ge(reloaded, RELOADS * DMA)
                pool.sem_inc(gathers_open, 1)

            def gather(dst, src, idx, k, bound, done_sem):
                pool.indirect_dma_start(
                    out=dst, out_offset=None, in_=src,
                    in_offset=bass.IndirectOffsetOnAxis(ap=idx[:, k:k + 1], axis=0),
                    bounds_check=bound, oob_is_err=False).then_inc(done_sem, DMA)

            def gather_src(g, s, it):
                wait(pool, one.src_loaded[s], GT * DMA * it)
                nc.gpsimd.tensor_copy(idx_now[:, s, 0, :], src_idx[:, bass.ds(g * GT, GT)]).then_inc(src_staged, 1)
                wait(pool, one.t_ready, GT * (g - 1))
                pool.wait_ge(src_staged, g + 1)
                pool.sem_inc(gathers_open, 1)
                for k in range(GT):
                    gather(src_rows_sb[:, s, k, :], x, idx_now[:, s, 0], k, N - 1, one.src_loaded[s])

            def gather_dst(g, s, it):
                wait(pool, one.dst_loaded[s], GT * DMA * it)
                nc.gpsimd.tensor_copy(idx_now[:, s, 1, :], rep_idx[:, bass.ds(g * GT, GT)]).then_inc(one.staged, 1)
                wait(pool, one.stored[s], DMA * it)
                pool.wait_ge(one.staged, g + 1)
                pool.sem_inc(gathers_open, 1)
                for k in range(GT):
                    gather(dst_rows_sb[:, s, k, :], x, idx_now[:, s, 1], k, N - 1, one.dst_loaded[s])

            def shift_head(g, s, it):
                pool.wait_ge(head_loaded[s], DMA * (it + 1))
                add_bias(nc.gpsimd, s, 0).then_inc(head_shifted, 1)

            def gathers_one(g, s, it):
                if is_group(g + 1):
                    gather_src(g + 1, 1 - s, it + s)
                gather_dst(g, s, it)
                if is_group(g + 1):
                    shift_head(g + 1, 1 - s, it + s)

            gather_src(0, 0, 0)
            pool.wait_ge(setup_done, 1)
            shift_head(0, 0, 0)
            every_group(pool, gathers_one)

            for s in range(2):
                pool.wait_ge(one_stored[s], DMA * GROUPS)
                pool.wait_ge(one.stored[s], DMA * GROUPS // 2)
            pool.wait_ge(match_done, GROUPS + 1)

            def gather_row(g, s, it):
                wait(pool, row_loaded[s], GT * DMA * it)
                nc.gpsimd.tensor_copy(idx_now[:, s, 0, :], row_idx[:, bass.ds(g * GT, GT)]).then_inc(row_staged, 1)
                pool.wait_ge(row_staged, g + 1)
                wait(pool, row_dotted, g - 1)
                pool.sem_inc(gathers_open, 1)
                for k in range(GT):
                    wait(pool, row_turned, GT * (g - 2) + k + 1)
                    pool.sem_inc(gathers_open, 1)
                    gather(src_rows_sb[:, s, k, :], table, idx_now[:, s, 0], k, N + EPAD - 1, row_loaded[s])

            pool.wait_ge(one.t_ready, TILES)
            for s in range(2):
                pool.wait_ge(one.src_loaded[s], GT * DMA * GROUPS // 2)
                pool.wait_ge(one.dst_loaded[s], GT * DMA * GROUPS // 2)
            every_group(pool, gather_row)

            for s in range(2):
                pool.wait_ge(two_stored[s], DMA * GROUPS)
                pool.wait_ge(row_loaded[s], GT * DMA * GROUPS // 2)

            def scatter(g, s, it):
                wait(pool, two.stored[s], GT * DMA * it)
                nc.gpsimd.tensor_copy(idx_now[:, s, 1, :], rep_idx[:, bass.ds(g * GT, GT)]).then_inc(two.staged, 1)
                pool.wait_ge(two.staged, g + 1)
                pool.sem_inc(gathers_open, 1)
                for k in range(GT):
                    pool.wait_ge(two.normed, GT * g + k + 1)
                    pool.sem_inc(gathers_open, 1)
                    pool.indirect_dma_start(
                        out=out, out_offset=bass.IndirectOffsetOnAxis(ap=idx_now[:, s, 1, k:k + 1], axis=0),
                        in_=finished[:, s * GT + k, :], in_offset=None,
                        bounds_check=N - 1, oob_is_err=False).then_inc(two.stored[s], DMA)

            every_group(pool, scatter)
            for s in range(2):
                pool.wait_ge(two.stored[s], GT * DMA * GROUPS // 2)

        @block.tensor
        def _(pe):
            pe.wait_ge(disorder_counted, 1)
            nc.tensor.matmul(ps_m[0:1, 0:1], disorder_by[:], ones_sum[:], start=True, stop=True).then_inc(disorder_counted, 1)
            pe.wait_ge(wide_ready, 1)
            for j in range(2):
                for h in range(HALVES):
                    last = nc.tensor.matmul(ps_y[:, j, 0:D], att_wide[:, 2 * j + h, :], w1_nat[:, h, :],
                                            start=h == 0, stop=h == HALVES - 1)
            last.then_inc(u_ready, 1)

            def scan_turns(n, *scans):
                pe.wait_ge(tails_ready, n + 1)
                for j, (row, tail) in enumerate(scans):
                    for h in range(2):
                        last = nc.tensor.transpose(tail_rows[j][:, h * HT:(h + 1) * HT], row[:, h, tail:tail + 1],
                                                   ident[0:HT, 0:HT])
                last.then_inc(tails_row, 1)
                pe.wait_ge(chain_ready, n + 1)
                for j, (row, tail) in enumerate(scans):
                    off = 0 if tail else 1
                    for h in range(2):
                        last = nc.tensor.transpose(carry_cols[j][:, h:h + 1],
                                                   chain_rows[:, j, off + h * HT:off + (h + 1) * HT], ident[0:1, 0:1])
                last.then_inc(chain_cols, 1)

            def to_lanes(n, row):
                pe.wait_ge(flip_ready, n + 1)
                for h in range(2):
                    last = nc.tensor.transpose(ps_m[:, h * HT:(h + 1) * HT], row[:, h, :], ident[0:HT, 0:HT])
                last.then_inc(flipped, 1)

            def to_rows(n, lanes):
                pe.wait_ge(flip_ready, n + 1)
                for h in range(2):
                    last = nc.tensor.transpose(ps_m[0:HT, h * P:(h + 1) * P], lanes[:, h * HT:(h + 1) * HT], ident[:])
                last.then_inc(flipped, 1)

            def wholes_to_row(n):
                pe.wait_ge(flip_ready, n + 1)
                for j, (row, tail) in enumerate(((lead_f, P - 1), (lead_r, 0))):
                    for h in range(2):
                        last = nc.tensor.transpose(ps_m[0:1, j * TILES + h * HT:j * TILES + (h + 1) * HT],
                                                   row[:, h, tail:tail + 1], ident[0:HT, 0:HT])
                last.then_inc(flipped, 1)

            wholes_to_row(0)
            scan_turns(0, (r_a, P - 1))
            to_lanes(1, r_f)

            def search(g, s):
                pe.wait_ge(one.select_ready, g + 1)
                wait(pe, match_done, g)
                for k in range(GT):
                    into = ps_d[:, k // 3, k % 3 * CODE:(k % 3 + 1) * CODE]
                    for n, (h, step) in enumerate(((0, step_hi), (0, step_lo), (1, step_hi), (1, step_lo))):
                        last = nc.tensor.matmul(into, below[:, h, s, k * P:(k + 1) * P], step[:, h, :],
                                                start=n == 0, stop=n == 3)
                last.then_inc(search_ready, 1)

            def slot_of(s, k):
                return (GT * s + k) % 2

            def project(g, s, k, w, t_copied, y_copied, stop):
                slot = slot_of(s, k)
                pe.wait_ge(t_copied, GT * g + k + 1)
                wait(pe, y_copied, GT * g + k - 1)
                for h in range(HALVES):
                    last = nc.tensor.matmul(ps_y[:, slot, 0:D], sums_t[:, slot, h * P:(h + 1) * P], w[:, h, :],
                                            start=h == 0, stop=stop and h == HALVES - 1)
                return last

            def add_one(g, s, it):
                search(g, s)
                pe.wait_ge(one.src_loaded[s], GT * DMA * (it + 1))

                def sums(k):
                    wait(pe, one.t_copied, GT * g + k - 1)
                    for h in range(HALVES):
                        last = nc.tensor.matmul(ps_t[:, slot_of(s, k), h * P:(h + 1) * P],
                                                src_rows_sb[:, s, k, h * P:(h + 1) * P],
                                                same[:, s, k * P:(k + 1) * P], start=True, stop=True)
                    last.then_inc(one.t_ready, 1)

                def finish(k):
                    slot = slot_of(s, k)
                    project(g, s, k, w0_sb, one.t_copied, one.y_copied, False)
                    nc.tensor.matmul(ps_y[:, slot, 0:D], same[:, s, k * P:(k + 1) * P], b0_all[:], start=False, stop=False)
                    wait(pe, one.y_copied, GT * g + k)
                    nc.tensor.matmul(ps_y[:, slot, 0:D], carries[:, s, k * P:(k + 1) * P], carried[:, 1 - slot, :],
                                     start=False, stop=True).then_inc(one.y_ready, 1)

                sums(0)
                for k in range(1, GT):
                    sums(k)
                    finish(k - 1)
                finish(GT - 1)

            every_group(pe, add_one)

            def finish(g, s, k):
                project(g, s, k, w1_sb, row_turn_copied, row_projected, True).then_inc(row_projecting, 1)

            def rows_of(g, s, it):
                pe.wait_ge(row_loaded[s], GT * DMA * (it + 1))

                def turn(k):
                    wait(pe, row_turn_copied, GT * g + k - 1)
                    for h in range(HALVES):
                        last = nc.tensor.transpose(ps_t[:, slot_of(s, k), h * P:(h + 1) * P],
                                                   src_rows_sb[:, s, k, h * P:(h + 1) * P], ident[:])
                    last.then_inc(row_turned, 1)

                for k in range(GT):
                    turn(k)
                    if k:
                        finish(g, s, k - 1)
                    elif is_group(g - 1):
                        finish(g - 1, 1 - s, GT - 1)

            pe.wait_ge(one.y_copied, TILES)
            pe.wait_ge(loaded, (SETUP_LOADS + 1) * DMA)
            wholes_to_row(2)
            to_rows(3, l_a)
            scan_turns(1, (r_b, 0))
            every_group(pe, rows_of)
            finish(GROUPS - 1, 1, GT - 1)

            to_rows(4, logit_l)
            scan_turns(2, (r_d, P - 1), (r_e, 0))
            scan_turns(3, (r_f, P - 1))
            pe.wait_ge(flip_ready, 6)
            for j, row in enumerate((r_a, r_b)):
                for h in range(2):
                    last = nc.tensor.transpose(ps_m[:, j * 256 + h * HT:j * 256 + (h + 1) * HT], row[:, h, :], ident[0:HT, 0:HT])
            last.then_inc(flipped, 1)

            def add_two(g, s, it):
                pe.wait_ge(two.select_ready, g + 1)
                pe.wait_ge(two.src_loaded[s], DMA * (it + 1))
                for k in range(GT):
                    slot = slot_of(s, k)
                    very_first = isinstance(g, int) and g == 0 and k == 0
                    wait(pe, two.y_copied, GT * g + k - 1)
                    last = nc.tensor.matmul(ps_y[:, slot, 0:D], same[:, s, k * P:(k + 1) * P], src_rows_sb[:, s, k, :],
                                            start=True, stop=very_first)
                    if not very_first:
                        pe.wait_ge(two.y_copied, GT * g + k)
                        before = proj[:, s * GT + k - 1, :] if k else carried[:, 0, :]
                        last = nc.tensor.matmul(ps_y[:, slot, 0:D], carries[:, s, k * P:(k + 1) * P], before,
                                                start=False, stop=True)
                    last.then_inc(two.y_ready, 1)

            every_group(pe, add_two)

        @block.scalar
        def _(act):
            def slot_of(s, k):
                return (GT * s + k) % 2

            def copies_one(g, s, k):
                if k < GT:
                    act.wait_ge(one.t_ready, GT * g + k + 1)
                    nc.scalar.copy(sums_t[:, slot_of(s, k), :], ps_t[:, slot_of(s, k), 0:D]).then_inc(one.t_copied, 1)
                if k:
                    slot = slot_of(s, k - 1)
                    act.wait_ge(one.y_ready, GT * g + k)
                    if k == 1:
                        wait(act, one.normed, g - 1)
                    nc.scalar.activation(proj[:, GT * s + k - 1, :], ps_y[:, slot, 0:D], ACT.Relu)
                    nc.scalar.copy(carried[:, slot, :], ps_y[:, slot, 0:D]).then_inc(one.y_copied, 1)

            def node_rstd(g):
                wait(act, last_normed, g)
                wait(act, x_normed, 2 * g)
                act.wait_ge(n_inv_ready, g + 1)
                nc.scalar.activation(n_rstd[:], n_inv[:], ACT.Sqrt).then_inc(n_rstd_ready, 1)

            def node_norm(g, s, it, r):
                if r == 0:
                    act.wait_ge(n_bias_ready, g + 1)
                    wait(act, one_stored[s], 2 * DMA * it)
                    wait(act, two_stored[s], 2 * DMA * it)
                nc.scalar.activation(x_one[:, s, r, :], x_in[:, s, r, :], ACT.Identity,
                                     bias=n_bias[:, 0, r:r + 1], scale=n_rstd[:, 0, r:r + 1])
                last = nc.scalar.activation(x_two[:, s, r, :], x_in[:, s, r, :], ACT.Identity,
                                            bias=n_bias[:, 1, r:r + 1], scale=n_rstd[:, 1, r:r + 1])
                if r in (HB - 1, RB - 2):
                    last.then_inc(x_normed, 1)

            def edge_rstd(ly, g, each):
                wait(act, ly.normed, each * g)
                act.wait_ge(ly.inv_ready, g + 1)
                nc.scalar.activation(e_rstd[:], e_inv[:], ACT.Sqrt).then_inc(ly.rstd_ready, 1)

            def edge_norm(g, s):
                act.wait_ge(one.bias_ready, g + 1)
                for k in range(GT):
                    last = nc.scalar.activation(dst_rows_sb[:, s, k, :], proj[:, GT * s + k, :], ACT.Identity,
                                                bias=e_bias[:, k:k + 1], scale=e_rstd[:, k:k + 1])
                last.then_inc(one.normed, 1)

            def turn_one(g, s, it):
                node_rstd(g)
                if is_group(g - 1):
                    edge_norm(g - 1, 1 - s)
                for k in range(GT):
                    if is_group(g + 1):
                        copies_one(g + 1, 1 - s, k)
                    if is_group(g + 1):
                        node_norm(g, s, it, 2 * k)
                        if k < GT - 1:
                            node_norm(g, s, it, 2 * k + 1)
                    else:
                        node_norm(g, s, it, k)
                if is_group(g + 1):
                    copies_one(g + 1, 1 - s, GT)
                edge_rstd(one, g, 1)

            act.wait_ge(setup_done, 1)
            for k in range(GT + 1):
                copies_one(0, 0, k)
            every_group(act, turn_one)
            edge_norm(GROUPS - 1, 1)

            def copy_row(g, s, k, it):
                act.wait_ge(row_projecting, GT * g + k + 1)
                if k == 0:
                    wait(act, row_kept[s], DMA * it)
                nc.scalar.copy(proj[:, GT * s + k, :], ps_y[:, slot_of(s, k), 0:D]).then_inc(row_projected, 1)

            def copies_rows(g, s, it):
                for k in range(GT):
                    act.wait_ge(row_turned, GT * g + k + 1)
                    nc.scalar.copy(sums_t[:, slot_of(s, k), :], ps_t[:, slot_of(s, k), 0:D]).then_inc(row_turn_copied, 1)
                    if k:
                        copy_row(g, s, k - 1, it)
                    elif is_group(g - 1):
                        copy_row(g - 1, 1 - s, GT - 1, 0)

            every_group(act, copies_rows)
            copy_row(GROUPS - 1, 1, GT - 1, 0)

            act.wait_ge(exp_ready, 1)
            nc.scalar.activation(r_e, r_e, ACT.Exp).then_inc(exp_done, 1)

            for s in range(2):
                act.wait_ge(one.stored[s], DMA * GROUPS // 2)
                act.wait_ge(row_kept[s], DMA * GROUPS // 2)

            def copy_two(g, s, k):
                wait(act, two.normed, GT * (g - 2) + k + 1)
                act.wait_ge(two.y_ready, GT * g + k + 1)
                last = nc.scalar.copy(proj[:, GT * s + k, :], ps_y[:, slot_of(s, k), 0:D])
                if k == GT - 1:
                    last = nc.scalar.copy(carried[:, 0, :], ps_y[:, slot_of(s, k), 0:D])
                last.then_inc(two.y_copied, 1)

            def norm_two(g, s, k):
                if k == 0:
                    act.wait_ge(two.bias_ready, g + 1)
                nc.scalar.activation(finished[:, s * GT + k, :], proj[:, GT * s + k, :], ACT.Identity,
                                     bias=e_bias[:, k:k + 1], scale=e_rstd[:, k:k + 1]).then_inc(two.normed, 1)

            def turn_two(g, s, it):
                for k in range(GT + 1):
                    if k < GT and is_group(g - 1):
                        norm_two(g - 1, 1 - s, k)
                    if k and is_group(g + 1):
                        copy_two(g + 1, 1 - s, k - 1)
                edge_rstd(two, g, GT)
                wait(act, two.stored[s], GT * DMA * it)

            for k in range(GT):
                copy_two(0, 0, k)
            every_group(act, turn_two)
            for k in range(GT):
                norm_two(GROUPS - 1, 1, k)

        @block.vector
        def _(dve):
            v = nc.vector
            steps = [0]

            def link(ins):
                steps[0] += 1
                ins.then_inc(dve_step, 1)
                dve.wait_ge(dve_step, steps[0])

            def link_all(instructions):
                for ins in instructions:
                    steps[0] += 1
                    ins.then_inc(dve_step, 1)
                dve.wait_ge(dve_step, steps[0])

            def seg_scan(n, *scans):
                ways = []
                for vals, into, reverse, biggest in scans:
                    flags = (ban_r if reverse else ban_f) if biggest else (keep_r if reverse else keep_f)
                    leads = (nolead_r if reverse else nolead_f) if biggest else (lead_r if reverse else lead_f)
                    start = -BIG if biggest else 0.0
                    ops = (ALU.add, ALU.max) if biggest else (ALU.mult, ALU.add)
                    way = slice(None, None, -1) if reverse else slice(None)
                    ways.append((into, leads, whole[:, 2 * biggest + reverse, :], start, ops, way, reverse))
                    for h in range(2):
                        last = v.tensor_tensor_scan(into[:, h, way], flags[:, h, way], vals[:, h, way], start, *ops)
                last.then_inc(tails_ready, 1)
                link_all(v.memset(chain_rows[:, j, TILES:TILES + 1] if reverse else chain_rows[:, j, 0:1], start)
                         for j, (into, leads, whole_row, start, ops, way, reverse) in enumerate(ways))
                dve.wait_ge(tails_row, n + 1)
                for j, (into, leads, whole_row, start, ops, way, reverse) in enumerate(ways):
                    row = chain_rows[:, j, 0:TILES] if reverse else chain_rows[:, j, 1:TILES + 1]
                    last = v.tensor_tensor_scan(row[:, way], whole_row[:, way], tail_rows[j][:, way], start, *ops)
                last.then_inc(chain_ready, 1)
                dve.wait_ge(chain_cols, n + 1)
                link_all(v.scalar_tensor_tensor(into[:, h, :], leads[:, h, :], carry_cols[j][:, h:h + 1], into[:, h, :], *ops)
                         for j, (into, leads, whole_row, start, ops, way, reverse) in enumerate(ways) for h in range(2))

            def copy_wholes(n):
                dve.wait_ge(flipped, n + 1)
                for j in range(2):
                    v.tensor_copy(whole[:, j, :], ps_m[0:1, j * TILES:(j + 1) * TILES])
                link_all(v.tensor_scalar(whole[:, 2 + j, :], ps_m[0:1, j * TILES:(j + 1) * TILES], 1.0, BIG,
                                         ALU.subtract, ALU.mult) for j in range(2))

            def order_edges():
                own = rank_f[:, 2, :]
                dve.wait_ge(before_ready, 2)
                v.tensor_copy(dst_score[:], dst_l[:]).then_inc(rank_step, 1)
                for h in range(2):
                    dve.wait_ge(half_loaded, DMA * (h + 1))
                    base = 1 + h * (1 + TILES + HT)
                    v.tensor_copy(half_line, half_line.bitcast(I32)).then_inc(rank_step, 1)
                    dve.wait_ge(rank_step, base + 1)

                    def count(t, done):
                        v.tensor_scalar(half_out, half_line, dst_score[:, bass.ds(t, 1)], None, ALU.is_lt, ALU.add,
                                        accum_out=rank_f[:, h, bass.ds(t, 1)]).then_inc(rank_step, 1)
                        dve.wait_ge(rank_step, done)

                    def count_own(n, first, start):
                        count(first + n - 1, start + 2 * n - 1)
                        tile = half_line[:, bass.ds((n - 1) * P, P)]
                        v.scalar_tensor_tensor(half_out[:, 0:P], tile, dst_score[:, bass.ds(first + n - 1, 1)], before_lane,
                                               ALU.is_equal, ALU.mult, accum_out=own[:, bass.ds(first + n - 1, 1)])
                        v.tensor_scalar(tile, tile, -0.5, None, ALU.add).then_inc(rank_step, 1)
                        dve.wait_ge(rank_step, start + 2 * n)

                    if h == 0:
                        with dve.Fori(1, HT + 1) as n:
                            count_own(n, 0, base + 1)
                        with dve.Fori(1, HT + 1) as n:
                            count(HT + n - 1, base + 1 + 2 * HT + n)
                    else:
                        with dve.Fori(1, HT + 1) as n:
                            count(n - 1, base + 1 + n)
                        with dve.Fori(1, HT + 1) as n:
                            count_own(n, HT, base + 1 + HT)
                    v.memset(e_tmp[:], 0.0).then_inc(half_ranked, 1)
                last = 1 + 2 * (1 + TILES + HT)
                v.tensor_tensor(own, own, rank_f[:, 0, :], ALU.add).then_inc(rank_step, 1)
                dve.wait_ge(rank_step, last + 1)
                v.tensor_tensor(rank_i, own, rank_f[:, 1, :], ALU.add).then_inc(ranked, 1)
                dve.wait_ge(reloaded, RELOADS * DMA)
                dve.wait_ge(refilled, 2)

            dve.wait_ge(loaded, SETUP_LOADS * DMA)
            dve.wait_ge(consts_ready, 8)
            link(v.memset(ones_sum[:], 1.0))
            link(v.tensor_tensor(r_a, a_prev, a_dst, ALU.is_gt))
            v.tensor_reduce(disorder_by[:], r_a, axis=mybir.AxisListType.XY, op=ALU.add).then_inc(disorder_counted, 1)
            dve.wait_ge(disorder_counted, 2)
            v.tensor_copy(disorder_sb[:], ps_m[0:1, 0:1]).then_inc(disorder_ready, 1)
            dve.wait_ge(disorder_ready, 1)
            dve_disorder = dve.value_load(disorder_sb[0:1, 0:1], min_val=0, max_val=EPAD)
            with dve.If(dve_disorder > 0):
                order_edges()
            link_all((
                v.tensor_scalar(relu_b0[:], b0_all[:], 0.0, None, ALU.max),
                v.tensor_tensor(keep_f, a_dst, a_prev, ALU.is_equal),
                v.tensor_tensor(keep_r, a_dst, a_next, ALU.is_equal),
                v.tensor_tensor(rep_l[:], dst_l[:], l_next, ALU.not_equal),
                v.tensor_copy(dst_u16, a_dst), v.tensor_copy(src_u16, a_src),
                v.tensor_scalar(src_next1[:], src_idx[:], 1.0, None, ALU.add),
                v.tensor_copy(tile_first[:], a_dst[:, :, 0]),
                v.tensor_scalar(r_b, a_dst, 1.0, None, ALU.add),
                v.tensor_scalar(r_c, a_up, 1.0, None, ALU.add),
                v.tensor_tensor(r_d, a_dst, a_next, ALU.not_equal),
                v.tensor_tensor(r_e, a_up, a_up_next, ALU.not_equal),
            ))
            v.tensor_copy(att_wide, att_cols[:].unsqueeze(2).to_broadcast([P, 4, P])).then_inc(wide_ready, 1)
            link_all(v.tensor_tensor_scan(into[:, h, way], keep[:, h, way], zeros_r[:, h, :], 1.0, ALU.mult, ALU.add)
                     for into, keep, way in ((lead_f, keep_f, slice(None)), (lead_r, keep_r, slice(None, None, -1)))
                     for h in range(2))
            v.memset(l_a, 0.0).then_inc(leads_ready, 1)
            dve.wait_ge(leads_ready, 1)
            v.memset(l_a, 0.0).then_inc(flip_ready, 1)
            link_all((v.tensor_tensor(r_b, r_b, r_d, ALU.mult), v.tensor_tensor(r_c, r_c, r_e, ALU.mult)))
            link(v.tensor_tensor(r_b, r_b, r_c, ALU.subtract))
            link(v.tensor_copy(r_int, r_b))
            link(v.tensor_single_scalar(r_int2, r_int, 255, ALU.bitwise_and))
            link(v.tensor_copy(r_c, r_int2))
            link_all((
                v.tensor_tensor(step_hi[:, :, 0:P], r_b, r_c, ALU.subtract),
                v.tensor_copy(step_lo[:, :, 0:P], r_c),
                v.tensor_copy(step_hi[:, :, P], code_sb[:, :, 0]),
                v.tensor_copy(step_lo[:, :, P], code_sb[:, :, 1]),
                v.tensor_scalar(l_a, rep_l[:], -1.0, -float(FAR), ALU.add, ALU.mult),
            ))
            link(v.tensor_tensor(rep_idx[:], l_a, dst_l[:], ALU.add))
            copy_wholes(0)
            seg_scan(0, (ones_r, r_a, 0, 0))
            v.tensor_copy(r_f, r_a).then_inc(flip_ready, 1)
            dve.wait_ge(flipped, 2)
            link(v.reciprocal(per_count[:], ps_m[:, 0:TILES]))
            dve.wait_ge(u_ready, 1)
            link_all((v.tensor_copy(u_src[:], ps_y[:, 0, 0:D]), v.tensor_copy(u_dst[:], ps_y[:, 1, 0:D])))
            v.reduce_sum(u_sum[:], u_dst[:], axis=mybir.AxisListType.X).then_inc(setup_done, 1)
            dve.wait_ge(setup_done, 1)

            def cols(a, g):
                return a[:, bass.ds(g * GT, GT)]

            def col(a, g, k):
                return a[:, bass.ds(g * GT + k, 1)]

            def selectors(g, s, it):
                dve.wait_ge(one.line_loaded[s], 3 * DMA * (it + 1))
                wait(dve, one.y_ready, GT * (g - 1))
                wait(dve, search_ready, g - 1)
                v.tensor_tensor(same[:, s, :].rearrange("p (k e) -> p k e", k=GT),
                                dst_line_sb[:, s, :].rearrange("p (k e) -> p k e", k=GT),
                                cols(dst_l, g).unsqueeze(2).to_broadcast([P, GT, P]), ALU.is_equal)
                for h in range(2):
                    last = v.tensor_scalar(below[:, h, s, :], src_line_sb[:, s, :], tile_first[:, h:h + 1], None, ALU.is_ge)
                last.then_inc(one.select_ready, 1)

            def nothing(step):
                pass

            def aggregate(stats, twice, gap, sq, part, stat, aggr, g, between=nothing):
                dve.wait_ge(stat, g + 1)
                v.tensor_tensor(twice[:], stats[:, :, 1], stats[:, :, 4], ALU.add)
                v.tensor_tensor(sq[:], stats[:, :, 2], stats[:, :, 5], ALU.add)
                v.tensor_tensor(gap[:], stats[:, :, 1], stats[:, :, 4], ALU.subtract).then_inc(aggr, 1)
                between(2)
                dve.wait_ge(aggr, 3 * g + 1)
                v.scalar_tensor_tensor(gap[:], gap[:], 0.25, gap[:], ALU.mult, ALU.mult).then_inc(aggr, 1)
                between(3)
                dve.wait_ge(aggr, 3 * g + 2)
                v.scalar_tensor_tensor(part[:], sq[:], 1.0 / D, gap[:], ALU.mult, ALU.add).then_inc(aggr, 1)
                between(4)
                dve.wait_ge(aggr, 3 * g + 3)

            def node_stats(g, s, it):
                dve.wait_ge(tail_loaded[s], DMA * (it + 1))
                add_bias(v, s, 1).then_inc(x_shifted, 1)
                dve.wait_ge(head_shifted, g + 1)
                dve.wait_ge(x_shifted, g + 1)
                for r in range(RB):
                    last = v.bn_stats(n_stats[:, r, :], x_in[:, s, r, :])
                last.then_inc(n_stat, 1)
                aggregate(n_stats, n_twice, n_gap, n_sq, n_part, n_stat, n_aggr, g)
                v.tensor_scalar(n_var[:, 0, :], n_part[:], EPS, None, ALU.add)
                v.tensor_scalar(n_var[:, 1, :], n_part[:], 1.0 + EPS, EPS * EPS, ALU.mult, ALU.add).then_inc(n_vars, 1)
                dve.wait_ge(n_vars, g + 1)
                v.reciprocal(n_inv[:], n_var[:]).then_inc(n_inv_ready, 1)

            def node_bias(g):
                wait(dve, last_normed, g)
                dve.wait_ge(n_rstd_ready, g + 1)
                v.scalar_tensor_tensor(n_bias[:], n_twice[:].unsqueeze(1).to_broadcast([P, 2, RB]), -0.5, n_rstd[:],
                                       ALU.mult, ALU.mult).then_inc(n_bias_ready, 1)

            def norm_last(g, s, it):
                wait(dve, one_stored[s], 2 * DMA * it)
                wait(dve, two_stored[s], 2 * DMA * it)
                dve.wait_ge(n_bias_ready, g + 1)
                for r in range(RB - 1 if is_group(g + 1) else HB, RB):
                    for j, into in enumerate((x_one, x_two)):
                        last = v.tensor_scalar(into[:, s, r, :], x_in[:, s, r, :], n_rstd[:, j, r:r + 1],
                                               n_bias[:, j, r:r + 1], ALU.mult, ALU.add)
                last.then_inc(last_normed, 1)

            def finish_stats(ly, g, s, between=nothing):
                for k in range(GT):
                    last = v.bn_stats(e_stats[:, k, :], proj[:, s * GT + k, :])
                last.then_inc(ly.stat, 1)
                between(1)
                aggregate(e_stats, e_twice, e_gap, e_sq, e_part, ly.stat, ly.aggr, g, between)
                v.tensor_scalar(e_var[:], e_part[:], EPS, None, ALU.add).then_inc(ly.vars, 1)
                between(5)
                dve.wait_ge(ly.vars, g + 1)
                v.reciprocal(e_inv[:], e_var[:]).then_inc(ly.inv_ready, 1)

            def finish_bias(ly, g):
                dve.wait_ge(ly.rstd_ready, g + 1)
                v.scalar_tensor_tensor(e_bias[:], e_twice[:], -0.5, e_rstd[:], ALU.mult, ALU.mult).then_inc(ly.bias_ready, 1)

            def finish_one(g, s, it):
                dve.wait_ge(one.y_copied, GT * (g + 1))
                dve.wait_ge(one.dst_loaded[s], GT * DMA * (it + 1))
                for k in range(GT):
                    row = proj[:, s * GT + k, :]
                    last = v.scalar_tensor_tensor(row, row, col(per_count, g, k), dst_rows_sb[:, s, k, :], ALU.mult, ALU.add)
                last.then_inc(one.summed, 1)
                node_bias(g)
                dve.wait_ge(one.summed, g + 1)
                for k in range(GT):
                    v.tensor_tensor_reduce(out=scrap[:, k, :], in0=proj[:, s * GT + k, :], in1=u_dst[:], scale=1.0, scalar=0.0,
                                           op0=ALU.mult, op1=ALU.add, accum_out=e_dot[:, 0, k:k + 1])
                finish_stats(one, g, s)

            def score_one(g):
                dve.wait_ge(one.rstd_ready, g + 1)
                v.tensor_tensor(e_tmp[:], e_dot[:, 0, :], e_rstd[:], ALU.mult)
                finish_bias(one, g)
                dve.wait_ge(one.bias_ready, g + 1)
                v.scalar_tensor_tensor(cols(dst_score, g), e_bias[:], u_sum[:], e_tmp[:], ALU.mult, ALU.add)

            def match(g):
                dve.wait_ge(search_ready, g + 1)
                for k in range(GT):
                    at = k % 3 * CODE
                    v.scalar_tensor_tensor(scrap[:, k, 0:P], ps_d[:, k // 3, at:at + P], col(src_next1, g, k), lane_code[:],
                                           ALU.is_equal, ALU.mult, accum_out=col(match_l, g, k))
                v.tensor_copy(code_l[:, bass.ds(g * GT, 6)].rearrange("p (a b) -> p a b", b=3),
                              ps_d[:, 0:2, 0:3 * CODE].rearrange("p a (b c) -> p a b c", c=CODE)[:, :, :, P])
                v.tensor_copy(col(code_l, g, 6), ps_d[:, 2, P:P + 1]).then_inc(match_done, 1)

            def turn_one(g, s, it):
                if is_group(g + 1):
                    selectors(g + 1, 1 - s, it + s)
                node_stats(g, s, it)
                if is_group(g - 1):
                    score_one(g - 1)
                finish_one(g, s, it)
                if not is_group(g + 1):
                    score_one(g)
                norm_last(g, s, it)
                if is_group(g + 1):
                    match(g + 1)

            selectors(0, 0, 0)
            match(0)
            every_group(dve, turn_one)

            link_all((v.tensor_scalar(weight_l[:], match_l[:], 0.0, None, ALU.is_gt),
                      v.scalar_tensor_tensor(per_total[:], match_l[:], -1.0, code_l[:], ALU.add, ALU.add)))
            link(v.tensor_tensor(per_total[:], per_total[:], src_idx[:], ALU.subtract))
            link(v.tensor_tensor(per_total[:], per_total[:], weight_l[:], ALU.mult))
            v.tensor_tensor(row_idx[:], per_total[:], src_idx[:], ALU.add).then_inc(match_done, 1)

            for s in range(2):
                dve.wait_ge(one_stored[s], DMA * GROUPS)
                dve.wait_ge(two_stored[s], DMA * GROUPS)
            link_all([v.tensor_scalar(ban, keep, 1.0, BIG, ALU.subtract, ALU.mult)
                      for ban, keep in ((ban_f, keep_f), (ban_r, keep_r), (nolead_f, lead_f), (nolead_r, lead_r))]
                     + [v.tensor_tensor(l_a, dst_score[:], rep_l[:], ALU.mult), v.tensor_copy(dst_float, dst_l[:])])
            v.memset(r_f, 0.0).then_inc(flip_ready, 1)
            copy_wholes(2)

            def rows_of_ps():
                return ps_m[0:HT, 0:2 * P].rearrange("p (h e) -> p h e", h=2)

            v.memset(r_c, 0.0).then_inc(flip_ready, 1)
            dve.wait_ge(flipped, 4)
            link(v.tensor_copy(r_a, rows_of_ps()))
            seg_scan(1, (r_a, r_b, 1, 0))

            def dots(g, s, it):
                dve.wait_ge(attr_loaded[s], DMA * (it + 1))
                attrs = attr_sb[:, s, :].rearrange("p (k f) -> p k f", k=GT)
                v.tensor_tensor(attrs, attrs, att_edge[:].unsqueeze(1).to_broadcast([P, GT, DE]), ALU.mult).then_inc(attr_scaled, 1)
                wait(dve, logit_done, g)
                dve.wait_ge(attr_scaled, g + 1)
                v.reduce_sum(e_tmp[:], attrs, axis=mybir.AxisListType.X)
                dve.wait_ge(row_loaded[s], GT * DMA * (it + 1))
                for k in range(GT):
                    last = v.tensor_tensor_reduce(out=scrap[:, k, :], in0=src_rows_sb[:, s, k, :], in1=u_src[:], scale=1.0,
                                                  scalar=0.0, op0=ALU.mult, op1=ALU.add, accum_out=e_dot[:, s, k:k + 1])
                last.then_inc(row_dotted, 1)
                dve.wait_ge(row_dotted, g + 1)
                v.tensor_tensor(cols(logit_l, g), e_dot[:, s, :], e_tmp[:], ALU.add).then_inc(logit_done, 1)

            every_group(dve, dots)
            dve.wait_ge(logit_done, GROUPS)

            v.memset(r_d, 0.0).then_inc(flip_ready, 1)
            dve.wait_ge(flipped, 5)
            link(v.tensor_tensor(r_c, rows_of_ps(), r_b, ALU.add))
            link(v.scalar_tensor_tensor(r_c, r_c, ALPHA, r_c, ALU.mult, ALU.max))
            seg_scan(2, (r_c, r_d, 0, 1), (r_c, r_e, 1, 1))
            link(v.tensor_tensor(r_d, r_d, r_e, ALU.max))
            v.tensor_tensor(r_e, r_c, r_d, ALU.subtract).then_inc(exp_ready, 1)
            dve.wait_ge(exp_done, 1)
            seg_scan(3, (r_e, r_f, 0, 0))
            v.tensor_copy(r_a, r_e)
            v.tensor_copy(r_b, r_f).then_inc(flip_ready, 1)
            dve.wait_ge(flipped, 6)
            v.tensor_copy(weight_l[:], ps_m[:, 0:TILES])
            link(v.scalar_tensor_tensor(per_total[:], ps_m[:, 256:256 + TILES], -1.0, rep_l[:], ALU.add, ALU.mult))
            link(v.tensor_scalar(per_total[:], per_total[:], 1.0, None, ALU.add))
            link(v.reciprocal(per_total[:], per_total[:]))

            def selector_two(g, s, it, k):
                if k == 0:
                    dve.wait_ge(two.line_loaded[s], 2 * DMA * (it + 1))
                    wait(dve, two.y_ready, GT * (g - 1))
                ins = v.tensor_scalar(same[:, s, k * P:(k + 1) * P], dst_line_sb[:, s, k * P:(k + 1) * P],
                                      col(dst_float, g, k), col(weight_l, g, k), ALU.is_equal, ALU.mult)
                if k == GT - 1:
                    ins.then_inc(two.select_ready, 1)

            def turn_two(g, s, it):
                if is_group(g - 1):
                    finish_bias(two, g - 1)

                def selector_ahead(k):
                    if is_group(g + 2):
                        selector_two(g + 2, s, it + 1, k)

                dve.wait_ge(two.y_copied, GT * (g + 1))
                dve.wait_ge(two.dst_loaded[s], DMA * (it + 1))
                for k in range(GT):
                    row = proj[:, s * GT + k, :]
                    last = v.scalar_tensor_tensor(row, row, col(per_total, g, k), dst_rows_sb[:, s, k, :],
                                                  ALU.mult, ALU.add)
                last.then_inc(two.summed, 1)
                selector_ahead(0)
                dve.wait_ge(two.summed, g + 1)
                finish_stats(two, g, s, selector_ahead)
                selector_ahead(GT - 1)

            for s in range(2):
                for k in range(GT):
                    selector_two(s, s, 0, k)
            every_group(dve, turn_two, 4)
            finish_bias(two, GROUPS - 1)


def kernel(x, src, dst, edge_attr_64, L0_gnn_W, L0_gnn_b, L1_gnn_W, L1_gnn_A):
    import concourse.bacc as bacc
    from concourse.bass_utils import run_bass_kernel_spmd

    def padded(a, before, after):
        return np.concatenate([np.asarray(before, np.int32),
                               np.asarray(a, np.int32), np.asarray(after, np.int32)])

    def lanes(line):
        return np.ascontiguousarray(line.reshape(TILES, P).T)

    src, dst = np.asarray(src), np.asarray(dst)
    src_line = padded(src, [], [0] * (EPAD - E))
    dst_line = padded(dst, [], [PAD_DST] * (EPAD - E))
    dst_framed = np.concatenate([np.full(P, -1, np.int32), dst_line, np.full(1, -1, np.int32)])
    code = N + np.arange(TILES) // GT * GE + np.arange(TILES) % GT
    step = np.diff(code, prepend=0)
    code_step = np.stack([step // 256 * 256, step % 256], -1).astype(np.float32).reshape(2, HT, 2).transpose(1, 0, 2)
    attr = np.concatenate([np.asarray(edge_attr_64), np.zeros((EPAD - E, DE), np.float32)])
    attr_lane = np.ascontiguousarray(attr.reshape(TILES, P, DE).transpose(1, 0, 2))
    w0, w1 = np.asarray(L0_gnn_W), np.asarray(L1_gnn_W)
    arrays = {
        "x": np.asarray(x), "src_line": src_line, "src_lane": lanes(src_line), "dst_framed": dst_framed,
        "dst_lane": lanes(dst_line), "dst_next_lane": lanes(dst_framed[P + 1:]),
        "code_step": np.ascontiguousarray(code_step), "attr_lane": attr_lane,
        "w0_t": np.ascontiguousarray(w0.T), "w1_t": np.ascontiguousarray(w1.T), "w1": w1,
        "b0": np.asarray(L0_gnn_b), "att": np.asarray(L1_gnn_A)[0],
    }
    nc = bacc.Bacc("TRN2", target_bir_lowering=False, num_devices=1)
    args = [nc.dram_tensor(name, a.shape, mybir.dt.from_np(a.dtype), kind="ExternalInput").ap()
            for name, a in arrays.items()]
    out = nc.dram_tensor("out", (N, D), F32, kind="ExternalOutput").ap()
    gnn_kernel(nc, *args, out)
    r = run_bass_kernel_spmd(nc, [arrays], core_ids=[0])
    return r.results[0]["out"]
```
